# Optimizing a Trainium2 kernel written in Bass

```python
import numpy as np
import jax
import jax.numpy as jnp

def _softmax(x, axis=-1):
    return jax.nn.softmax(x, axis=axis)

def _gelu(x):
    return jax.nn.gelu(x, approximate=True)

def _silu(x):
    return jax.nn.silu(x)

def _sigmoid(x):
    return jax.nn.sigmoid(x)

def _layernorm(x, axis=-1, eps=1e-05):
    m = jnp.mean(x, axis=axis, keepdims=True)
    v = jnp.var(x, axis=axis, keepdims=True)
    return (x - m) / jnp.sqrt(v + eps)

def _scatter_add(tgt, idx, src, axis=0):
    return tgt.at[idx].add(src)

def _segment_sum(src, seg, n):
    return jax.ops.segment_sum(src, seg, n)
kernel_name = 'mk_adj_resnorm_d2_adj_r2_d476c8'

def setup_inputs(seed: int=0):
    np.random.seed(seed)
    _w = jnp.asarray

    def _rec_inputs():
        import jax
        import jax.numpy as jnp
        _gk = jax.random.key(seed)
        x = -0.0001538 + 1 * jax.random.normal(jax.random.fold_in(_gk, 1), (64, 128, 384), jnp.float32)
        _a = jax.random.bernoulli(jax.random.fold_in(_gk, 2), 0.125, (64, 128, 128))
        _a = jnp.logical_or(_a, jnp.eye(128, dtype=bool))
        adj = _a
        return (x, adj)
    x, adj = _rec_inputs()

    def _L0_gnn_setup():
        import jax, jax.numpy as jnp
        import numpy as np
        B, S, H = (4, 1024, 384)
        NUM_HEADS = 6
        HEAD_SIZE = H // NUM_HEADS
        NEG = -9000000000000000.0

        def _heads(x):
            b, s, _ = x.shape
            return x.reshape(b, s, NUM_HEADS, HEAD_SIZE).transpose(0, 2, 1, 3)
        key = jax.random.key(seed)
        ks = jax.random.split(key, 10)
        seq_inputs = jax.random.normal(ks[0], (B, S, H), dtype=jnp.float32)
        gm = jax.random.randint(ks[1], (B, S, S), 0, 2) > 0
        graph_mask = gm | jnp.eye(S, dtype=bool)[None]
        sc = 1.0 / np.sqrt(H)
        Wq = jax.random.normal(ks[2], (H, H), dtype=jnp.float32) * sc
        bq = jnp.zeros((H,), dtype=jnp.float32)
        Wk = jax.random.normal(ks[3], (H, H), dtype=jnp.float32) * sc
        bk = jnp.zeros((H,), dtype=jnp.float32)
        Wv = jax.random.normal(ks[4], (H, H), dtype=jnp.float32) * sc
        bv = jnp.zeros((H,), dtype=jnp.float32)
        Wf = jax.random.normal(ks[5], (H, H), dtype=jnp.float32) * sc
        bf = jnp.zeros((H,), dtype=jnp.float32)
        return {'seq_inputs': seq_inputs, 'Wq': Wq, 'bq': bq, 'Wk': Wk, 'bk': bk, 'Wv': Wv, 'bv': bv, 'Wf': Wf, 'bf': bf, 'graph_mask': graph_mask}
    _L0_gnn_all = _L0_gnn_setup()
    _L0_gnn_in = {k: v for k, v in _L0_gnn_all.items() if k in ('Wq', 'bq', 'Wk', 'bk', 'Wv', 'bv', 'Wf', 'bf')}
    del _L0_gnn_all

    def _L1_gnn_setup():
        import jax, jax.numpy as jnp
        import numpy as np
        ATT_HEAD = 12
        IN_DIM = 384
        OUT_DIM = IN_DIM // ATT_HEAD
        LEAKY_ALPHA = 0.2
        B, N = (8, 256)
        key = jax.random.key(seed)
        ks = jax.random.split(key, 8)
        feat_in = jax.random.normal(ks[0], (B, N, IN_DIM), dtype=jnp.float32)
        adj = jax.random.randint(ks[1], (B, N, N), 0, 2) > 0
        lim_W = float(np.sqrt(6.0 / (IN_DIM + OUT_DIM)))
        W = jax.random.uniform(ks[2], (ATT_HEAD, IN_DIM, OUT_DIM), minval=-lim_W, maxval=lim_W, dtype=jnp.float32)
        b = jnp.zeros((OUT_DIM,), dtype=jnp.float32)
        lim_w = float(np.sqrt(6.0 / (OUT_DIM + 1)))
        w_src = jax.random.uniform(ks[3], (ATT_HEAD, OUT_DIM, 1), minval=-lim_w, maxval=lim_w, dtype=jnp.float32)
        w_dst = jax.random.uniform(ks[4], (ATT_HEAD, OUT_DIM, 1), minval=-lim_w, maxval=lim_w, dtype=jnp.float32)
        std_H = float(np.sqrt(2.0 / (IN_DIM + IN_DIM)))
        H_w = jax.random.normal(ks[5], (IN_DIM, IN_DIM), dtype=jnp.float32) * std_H
        H_b = jax.random.normal(ks[6], (IN_DIM,), dtype=jnp.float32) * 0.01
        return {'feat_in': feat_in, 'adj': adj, 'W': W, 'b': b, 'w_src': w_src, 'w_dst': w_dst, 'H_w': H_w, 'H_b': H_b}
    _L1_gnn_all = _L1_gnn_setup()
    _L1_gnn_in = {k: v for k, v in _L1_gnn_all.items() if k in ('W', 'b', 'w_src', 'w_dst', 'H_w', 'H_b')}
    del _L1_gnn_all
    return {'x': x, 'adj': adj, 'L0_gnn_Wq': _L0_gnn_in['Wq'], 'L0_gnn_bq': _L0_gnn_in['bq'], 'L0_gnn_Wk': _L0_gnn_in['Wk'], 'L0_gnn_bk': _L0_gnn_in['bk'], 'L0_gnn_Wv': _L0_gnn_in['Wv'], 'L0_gnn_bv': _L0_gnn_in['bv'], 'L0_gnn_Wf': _L0_gnn_in['Wf'], 'L0_gnn_bf': _L0_gnn_in['bf'], 'L1_gnn_W': _L1_gnn_in['W'], 'L1_gnn_b': _L1_gnn_in['b'], 'L1_gnn_w_src': _L1_gnn_in['w_src'], 'L1_gnn_w_dst': _L1_gnn_in['w_dst'], 'L1_gnn_H_w': _L1_gnn_in['H_w'], 'L1_gnn_H_b': _L1_gnn_in['H_b']}

def reference(x, adj, L0_gnn_Wq, L0_gnn_bq, L0_gnn_Wk, L0_gnn_bk, L0_gnn_Wv, L0_gnn_bv, L0_gnn_Wf, L0_gnn_bf, L1_gnn_W, L1_gnn_b, L1_gnn_w_src, L1_gnn_w_dst, L1_gnn_H_w, L1_gnn_H_b):
    import jax
    import jax.numpy as jnp

    def _L0_gnn_ref(seq_inputs, Wq, bq, Wk, bk, Wv, bv, Wf, bf, graph_mask):
        import jax, jax.numpy as jnp
        import numpy as np
        B, S, H = (4, 1024, 384)
        NUM_HEADS = 6
        HEAD_SIZE = H // NUM_HEADS
        NEG = -9000000000000000.0

        def _heads(x):
            b, s, _ = x.shape
            return x.reshape(b, s, NUM_HEADS, HEAD_SIZE).transpose(0, 2, 1, 3)
        q = _heads(seq_inputs @ Wq + bq)
        k = _heads(seq_inputs @ Wk + bk)
        v = _heads(seq_inputs @ Wv + bv)
        scores = jnp.einsum('bhqd,bhkd->bhqk', q, k) / np.sqrt(HEAD_SIZE)
        bias = jnp.where(graph_mask, 0.0, NEG)[:, None]
        probs = jax.nn.softmax(scores + bias, axis=-1)
        ctx = jnp.einsum('bhqk,bhkd->bhqd', probs, v)
        ctx = ctx.transpose(0, 2, 1, 3).reshape(seq_inputs.shape[0], seq_inputs.shape[1], H)
        return ctx @ Wf + bf

    def _L1_gnn_ref(feat_in, adj, W, b, w_src, w_dst, H_w, H_b):
        import jax, jax.numpy as jnp
        import numpy as np
        ATT_HEAD = 12
        IN_DIM = 384
        OUT_DIM = IN_DIM // ATT_HEAD
        LEAKY_ALPHA = 0.2
        B, N = (8, 256)
        h = jnp.einsum('bnd,ade->bane', feat_in, W)
        th = jnp.tanh(h)
        attn_src = jnp.einsum('bane,aeo->bano', th, w_src)
        attn_dst = jnp.einsum('bane,aeo->bano', th, w_dst)
        attn = attn_src + jnp.swapaxes(attn_dst, 2, 3)
        attn = jnp.where(attn >= 0, attn, LEAKY_ALPHA * attn)
        mask = ~adj[:, None, :, :]
        attn = jnp.where(mask, jnp.float32(-999.0), attn)
        attn = jax.nn.softmax(attn, axis=-1)
        feat_out = jnp.einsum('banm,bame->bane', attn, h) + b
        feat_out = jnp.swapaxes(feat_out, 1, 2).reshape(feat_in.shape[0], feat_in.shape[1], -1)
        feat_out = jax.nn.elu(feat_out)
        gate = jax.nn.sigmoid(feat_in @ H_w.T + H_b)
        return gate * feat_out + (1.0 - gate) * feat_in
    x = _layernorm(x + _L0_gnn_ref(x, L0_gnn_Wq, L0_gnn_bq, L0_gnn_Wk, L0_gnn_bk, L0_gnn_Wv, L0_gnn_bv, L0_gnn_Wf, L0_gnn_bf, adj), axis=-1)
    x = _layernorm(x + _L1_gnn_ref(x, adj, L1_gnn_W, L1_gnn_b, L1_gnn_w_src, L1_gnn_w_dst, L1_gnn_H_w, L1_gnn_H_b), axis=-1)
    return x

_drawn_inputs = setup_inputs


def setup_inputs(seed=0):
    import zlib

    import numpy as np

    out = dict(_drawn_inputs(seed))
    spreads = {'L0_gnn_bq': (0.0, 0.276),
     'L0_gnn_bk': (0.0, 2.0),
     'L0_gnn_bv': (0.0, 0.1),
     'L0_gnn_bf': (0.0, 0.1),
     'L1_gnn_b': (0.0, 0.1)}
    factors = {'L1_gnn_H_b': 35.193}
    for name, (base, spread) in spreads.items():
        noise = np.random.default_rng([zlib.crc32(name.encode()), seed]).standard_normal(out[name].shape)
        drawn = base * np.exp(spread * noise) if base else spread * noise
        out[name] = jnp.asarray(drawn.astype(out[name].dtype))
    for name, factor in factors.items():
        out[name] = (out[name] * factor).astype(out[name].dtype)
    return out
```

```python
from contextlib import ExitStack

import concourse.bass as bass
from concourse import mybir

ALU = mybir.AluOpType
ACT = mybir.ActivationFunctionType
F32 = mybir.dt.float32
F32R = mybir.dt.float32r
BF16 = mybir.dt.bfloat16
AX_X = mybir.AxisListType.X

B, N, D = 64, 128, 384
P = 128
C = D // P
G = 4
NG = B // G
H0, D0 = 6, 64
H1, D1 = 12, 32
E1 = D1 + 1
EPS = 1e-5
HI_LO = ((0, 0), (1, 0), (0, 1))


def build_program(nc, x, adj, Wq, bq, Wk, bk, Wv, bv, Wf, bf, W1, b1, w_src, w_dst, HwT, Hb,
                  ident_in, block_in, pick_in, out):
    with ExitStack() as ctx:
        def sb(name, shape, dt=F32):
            return ctx.enter_context(nc.sbuf_tensor(name, shape, dt))

        def psum(name, shape, dt=F32):
            return ctx.enter_context(nc.psum_tensor(name, shape, dt))

        def sem(name):
            return ctx.enter_context(nc.semaphore(name))

        ps_a = psum("ps_a", [P, 512])
        ps_b = psum("ps_b", [P, 512])
        ps_s = psum("ps_s", [P, 2, 512])
        ps_c = psum("ps_c", [P, 512])
        ps_d = psum("ps_d", [P, 3, 512])

        ident = sb("ident", [P, P])
        ident_b = sb("ident_b", [P, P], BF16)
        ident_53 = sb("ident_53", [P, P], BF16)
        ident_100 = sb("ident_100", [P, P], BF16)
        block = sb("block", [P, C, H1])
        pick_b = sb("pick_b", [3 * H1, H1, P], BF16)
        ones_b = sb("ones_b", [3, P], BF16)
        minus_half = sb("minus_half", [P, 1])
        w_parts = {n: [sb(f"{n}_hi", [P, C, D], F32R), sb(f"{n}_lo", [P, C, D], F32R)]
                   for n in ("wq", "wk", "wv", "wf", "w1", "hw")}
        bq_col = sb("bq_col", [P, C])
        bq8 = sb("bq8", [P, C])
        bk_col = sb("bk_col", [P, C])
        bv_all = sb("bv_all", [P, D])
        bf_all = sb("bf_all", [P, D])
        b1_all = sb("b1_all", [P, D1])
        w_cols = sb("w_cols", [P, 2, C])
        w_sd = sb("w_sd", [P, C, 2, H1])
        hb_row = sb("hb_row", [1, D])
        hb_rest = sb("hb_rest", [1, 2, D])
        hb_split = sb("hb_split", [1, 3, D], BF16)
        hb_rows = sb("hb_rows", [3, D], BF16)
        mask = sb("mask", [P, B, N], BF16)

        x_in = sb("x_in", [P, G, D])
        xT = [sb("xT_hi", [P, C, G * N], F32R), sb("xT_lo", [P, C, G * N], F32R)]
        xb = sb("xb", [P, 2, G, D])
        qT = sb("qT", [P, 2, C, G * N])
        kT = sb("kT", [P, 2, C, G * N])
        v = sb("v", [P, 2, G, D])
        p0 = sb("p0", [P, 2, C, N])
        p0T = sb("p0T", [P, 2, C, N])
        ctxT = [sb("ctxT_hi", [P, C, N], F32R), sb("ctxT_lo", [P, C, N], F32R)]
        r0 = sb("r0", [P, D])
        s0 = sb("s0", [P, 64])
        max0, neg0, sum0, inv0 = (s0[:, 8 * k:8 * k + H0] for k in range(4))
        st0, mv0, ve0, rs0, nm0 = s0[:, 32:38], s0[:, 40:42], s0[:, 44:45], s0[:, 46:47], s0[:, 48:49]
        x1 = sb("x1", [P, 2, G, D])
        x1T = [sb("x1T_hi", [P, C, N], F32R), sb("x1T_lo", [P, C, N], F32R)]
        h = sb("h", [P, 2, H1, E1])
        th = sb("th", [P, D])
        gate = sb("gate", [P, 2, D])
        thT = sb("thT", [P, C, N])
        sd = sb("sd", [P, 2, 2, H1])
        dst_rest = sb("dst_rest", [P, 2, H1])
        dst3 = sb("dst3", [P, 3, H1], BF16)
        dT = sb("dT", [3 * H1, N], BF16)
        z = sb("z", [P, H1, N])
        s1 = sb("s1", [P, 64])
        dmax, zmax, m1, neg1 = (s1[:, 12 * k:12 * k + H1] for k in range(4))
        p1T = sb("p1T", [P, H1, N])
        s2 = sb("s2", [P, 64])
        inv1 = s2[:, 0:12]
        st1, mv1, ve1, rs1, nm1 = s2[:, 16:22], s2[:, 24:26], s2[:, 28:29], s2[:, 30:31], s2[:, 32:33]
        f = sb("f", [P, H1, D1])
        fe = sb("fe", [P, H1, D1])
        r1 = sb("r1", [P, D])
        y = sb("y", [P, 2, D])
        stage = [z[:, :, :].rearrange("p a n -> p (a n)")[:, 0:C * D].rearrange("p (c n) -> p c n", c=C),
                 p1T[:, :, :].rearrange("p a n -> p (a n)")[:, 0:C * D].rearrange("p (c n) -> p c n", c=C)]
        x1_flat = x1[:].rearrange("p a j d -> p (a j d)")
        pick = x1_flat[0:3 * H1, 0:H1 * P].rearrange("p (a n) -> p a n", a=H1)
        adj_u8 = x1_flat[:, 1536:1536 + B * N // 16].bitcast(mybir.dt.uint8).rearrange("p (b n) -> p b n", n=N)

        names = """ident_in_ready const_in weight_in_0 weight_in_1 adj_in x_in_ready weight_hi weight_lo mask_ready consts_ready pick_ready hb_moved
            bias_ready wsd_ready stage_free x_turned x_hi x_lo xb_ready q_made q_ready k_made k_ready v_made v_ready
            scores_ready att_small neg_ready exp0_ready inv0_ready p0_ready p0_turned p0T_even p0T_odd
            ctx_made ctx_hi ctx_lo out_made r0_ready mv0_ready ln0_small x1_ready
            x1_turned x1_hi x1_lo h_made h_ready th_ready gate_made gate_ready th_turned thT_ready sd_made
            sd_ready split_small dst3_ready d_turned dT_ready logits_ready dmax_ready z_ready max1_small neg1_ready
            leaky_ready exp1_ready p1_turned p1T_0 p1T_1 p1T_2 ph_made inv1_ready f0_ready f1_ready
            fm_ready fe_ready tail_small r1_ready mv1_ready ln1_small y_ready y_stored_0 y_stored_1"""
        S = {n: sem(n) for n in names.split()}

        def wait(eng, name, value):
            if not isinstance(value, int) or value > 0:
                eng.wait_ge(S[name], value)

        def wait_apart(eng, name, value):
            if not isinstance(value, int):
                value = eng.to_reg(value)
                eng.wait_ge(S["ident_in_ready"], 16)
            wait(eng, name, value)

        W_ORDER = ["wq", "wk", "wv", "wf", "w1", "hw"]
        DRAM_W = {"wq": Wq, "wk": Wk, "wv": Wv, "wf": Wf, "hw": HwT}
        x_dram = x.rearrange("(g b) n d -> g n b d", b=G)
        adj_dram = adj.rearrange("(s b) n m -> s n b m", b=B // 4)
        out_dram = out

        def pipeline(eng, iteration):
            for g in (0, 1, 2):
                iteration(g, g % 2, g)
            with eng.Fori(0, (NG - 4) // 2) as pair:
                iteration(pair * 2 + 3, 1, 3)
                iteration(pair * 2 + 4, 0, 4)
            for g in range(NG - 1, NG + 3):
                iteration(g, g % 2, g)

        def parts(n):
            return n < NG, 1 <= n <= NG, 2 <= n <= NG + 1

        def has_tail(n, j, lag=1):
            return 0 <= G * (n - 2) + j - lag < B

        block_ = ctx.enter_context(nc.Block())

        @block_.sync
        def _(sp):
            sp.dma_start(x_in[:], x_dram[0]).then_inc(S["x_in_ready"], 16)
            sp.dma_start(ident[:], ident_in).then_inc(S["ident_in_ready"], 16)
            for n, name in enumerate(W_ORDER):
                wait(sp, "weight_hi", n - 1)
                wait(sp, "weight_lo", n - 1)
                if name == "w1":
                    for c in range(C):
                        sp.dma_start(stage[n % 2][:, c, :].rearrange("p (a e) -> p a e", a=H1),
                                     W1[:, c * P:(c + 1) * P, :].rearrange("a p e -> p a e")
                                     ).then_inc(S[f"weight_in_{n % 2}"], 16)
                else:
                    for c in range(C):
                        sp.dma_start(stage[n % 2][:, c, :],
                                     DRAM_W[name][c * P:(c + 1) * P, :]).then_inc(S[f"weight_in_{n % 2}"], 16)
            def iteration(g, par, n):
                qkv, att, gat = parts(n)
                for j in range(G):
                    if has_tail(n, j, 2):
                        t = G * (g - 2) + j - 2
                        wait(sp, "y_ready", t + 1)
                        dst = out_dram[t] if isinstance(t, int) else out_dram[bass.ds(t, 1)].rearrange("o n d -> (o n) d")
                        sp.dma_start(dst, y[:, j % 2, :]).then_inc(S[f"y_stored_{j % 2}"], 16)
                    if j == 2 and n + 1 < NG:
                        wait(sp, "xb_ready", G * (g + 1))
                        wait(sp, "x_lo", G * (g + 1))
                        sp.dma_start(x_in[:], x_dram[g + 1] if isinstance(g, int)
                                     else x_dram[bass.ds(g + 1, 1)].rearrange("o n b d -> (o n) b d")
                                     ).then_inc(S["x_in_ready"], 16)
            pipeline(sp, iteration)
            for k in range(2):
                sp.wait_ge(S[f"y_stored_{k}"], 16 * B // 2)

        @block_.tensor
        def _(pe):
            def split_product(out_ap, lhs, rhs):
                for c in range(C):
                    for k, (a, b) in enumerate(HI_LO):
                        last = pe.matmul(out_ap, lhs(a, c), rhs(b, c), start=(c == 0 and k == 0),
                                         stop=(c == C - 1 and k == 2))
                return last

            def turn_x(g):
                wait(pe, "x_in_ready", 16 * (g + 1))
                wait(pe, "v_ready", G * g)
                wait(pe, "ctx_lo", G * (g - 1))
                wait(pe, "r0_ready", G * (g - 1))
                for j in range(G):
                    if j >= 2:
                        wait(pe, "x_lo", G * g + j - 1)
                    bank = (ps_a, ps_b)[j % 2]
                    for c in range(C):
                        last = pe.transpose(bank[:, c * P:(c + 1) * P], x_in[:, j, c * P:(c + 1) * P], ident[:])
                    last.then_inc(S["x_turned"], 1)

            def project_qk(name, m, bank, made):
                split_product(bank[:], lambda a, c: w_parts[name][a][:, c, m * P:(m + 1) * P],
                              lambda b, c: xT[b][:, c, :]).then_inc(S[made], 1)

            def project_v(j, bank):
                split_product(bank[:, 0:D], lambda a, c: xT[a][:, c, j * N:(j + 1) * N],
                              lambda b, c: w_parts["wv"][b][:, c, :]).then_inc(S["v_made"], 1)

            def fill(g, n, j, bank):
                att = parts(n)[1]
                ta = G * (g - 1) + j
                if j == 0:
                    wait(pe, "x_lo", G * (g + 1))
                elif att and bank == "a":
                    wait(pe, "ctx_lo", ta)
                if j > 0 and att and (bank == "b" or j == 3):
                    wait(pe, "r0_ready", ta)
                if j == 0 and bank == "a":
                    if n == 0:
                        wait(pe, "weight_lo", 1)
                    project_qk("wq", 0, ps_a, "q_made")
                elif j == 0:
                    project_qk("wq", 1, ps_b, "q_made")
                elif j == 1 and bank == "a":
                    wait(pe, "q_ready", 3 * g + 1)
                    project_qk("wq", 2, ps_a, "q_made")
                elif j == 1:
                    wait(pe, "q_ready", 3 * g + 2)
                    if n == 0:
                        wait(pe, "weight_lo", 2)
                    project_qk("wk", 0, ps_b, "k_made")
                elif j == 2 and bank == "a":
                    wait(pe, "q_ready", 3 * g + 3)
                    project_qk("wk", 1, ps_a, "k_made")
                elif j == 2:
                    wait(pe, "k_ready", 3 * g + 1)
                    project_qk("wk", 2, ps_b, "k_made")
                elif bank == "a":
                    if n == 0:
                        wait(pe, "weight_lo", 3)
                    wait(pe, "k_ready", 3 * g + 2)
                    project_v(0, ps_a)
                    wait(pe, "k_ready", 3 * g + 3)
                    project_v(1, ps_b)
                else:
                    wait(pe, "v_ready", G * g + 1)
                    project_v(2, ps_a)
                    wait(pe, "v_ready", G * g + 2)
                    project_v(3, ps_b)

            def scores(t, g, par, j):
                wait(pe, "p0T_even", t)
                wait(pe, "p0T_odd", t)
                if j == 0:
                    wait(pe, "q_ready", 3 * g)
                    wait(pe, "k_ready", 3 * g)
                m = mask[:, t, :].unsqueeze(1) if isinstance(t, int) else mask[:, bass.ds(t, 1), :]
                for o in range(2):
                    pe.matmul(ps_s[:, o, 0:C * N].rearrange("p (i n) -> p i n", i=C), ident_53[:],
                              m.broadcast_to([P, C, N]), start=True, stop=False)
                for i in range(C):
                    for o in range(2):
                        q_, k_ = (w[D0 * o:D0 * (o + 1), par, i, j * N:(j + 1) * N] for w in (qT, kT))
                        last = pe.matmul(ps_s[:, o, i * N:(i + 1) * N], q_, k_, start=False, stop=(i == C - 1))
                last.then_inc(S["scores_ready"], 1)

            def turn_p0(t):
                wait(pe, "p0_ready", t + 1)
                for o in range(2):
                    for i in range(C):
                        last = pe.transpose(ps_s[:, o, i * N:(i + 1) * N], p0[:, o, i, :], ident[:])
                last.then_inc(S["p0_turned"], 1)

            def context(t, g, par, j, n):
                if j == 0:
                    wait(pe, "v_ready", G * g)
                if parts(n)[0]:
                    name, count = (("q_ready", 3 * g + 1), ("q_ready", 3 * g + 3),
                                   ("k_ready", 3 * g + 2), ("v_ready", G * g + 3))[j]
                    wait(pe, name, count)
                else:
                    wait(pe, "ctx_lo", t)
                wait(pe, "p0T_even", t + 1)
                wait(pe, "p0T_odd", t + 1)
                for o in range(2):
                    for i in range(C):
                        hd = 2 * i + o
                        last = pe.matmul(ps_a[D0 * o:D0 * (o + 1), i * N:(i + 1) * N],
                                         v[:, par, j, hd * D0:(hd + 1) * D0], p0T[:, o, i, :], start=True, stop=True)
                last.then_inc(S["ctx_made"], 1)

            def project_out(t, g, j, n):
                if parts(n)[0]:
                    name, count = (("q_ready", 3 * g + 2), ("k_ready", 3 * g + 1),
                                   ("k_ready", 3 * g + 3), ("v_ready", G * g + 4))[j]
                    wait(pe, name, count)
                else:
                    wait(pe, "r0_ready", t)
                wait(pe, "ctx_lo", t + 1)
                if n == 1 and j == 0:
                    wait(pe, "weight_lo", 4)
                split_product(ps_b[:, 0:D], lambda a, c: ctxT[a][:, c, :],
                              lambda b, c: w_parts["wf"][b][:, c, :]).then_inc(S["out_made"], 1)

            def turn_x1(t, par, j):
                wait(pe, "f0_ready", t - 1)
                wait(pe, "x1_ready", t + 1)
                for c in range(C):
                    last = pe.transpose(ps_c[:, c * P:(c + 1) * P], x1[:, par, j, c * P:(c + 1) * P], ident[:])
                last.then_inc(S["x1_turned"], 1)

            def project_h_gate(t, n, j):
                wait(pe, "x1_lo", t + 1)
                wait(pe, "z_ready", t)
                if n == 2 and j == 0:
                    wait(pe, "weight_lo", 6)
                    wait(pe, "hb_moved", 16)
                    wait(pe, "pick_ready", 1)
                split_product(ps_d[:, 1, 0:D], lambda a, c: x1T[a][:, c, :],
                              lambda b, c: w_parts["w1"][b][:, c, :]).then_inc(S["h_made"], 1)
                for c in range(C):
                    for a, b in HI_LO:
                        pe.matmul(ps_d[:, 2, 0:D], x1T[a][:, c, :], w_parts["hw"][b][:, c, :],
                                  start=(c == 0 and (a, b) == HI_LO[0]), stop=False)
                pe.matmul(ps_d[:, 2, 0:D], ones_b[:], hb_rows[:], start=False, stop=True).then_inc(S["gate_made"], 1)

            def turn_th(t):
                wait(pe, "th_ready", t + 1)
                for c in range(C):
                    last = pe.transpose(ps_c[:, c * P:(c + 1) * P], th[:, c * P:(c + 1) * P], ident[:])
                last.then_inc(S["th_turned"], 1)

            def src_dst(t, n, j):
                wait(pe, "thT_ready", t + 1)
                if n == 2 and j == 0:
                    wait(pe, "wsd_ready", 2)
                for c in range(C):
                    last = pe.matmul(ps_c[:, 0:2 * H1], thT[:, c, :], w_sd[:, c, :, :].rearrange("p s a -> p (s a)"),
                                     start=(c == 0), stop=(c == C - 1))
                last.then_inc(S["sd_made"], 1)

            def turn_dst(t):
                wait_apart(pe, "sd_ready", t + 1)
                wait(pe, "dst3_ready", t + 1)
                pe.transpose(ps_c[0:3 * H1, 0:N // 2].bitcast(BF16), dst3[:, :, :].rearrange("p s a -> p (s a)"),
                             ident_b[:]).then_inc(S["d_turned"], 1)

            def logits(t):
                for q, reader in ((0, "p1T_0"), (1, "p1T_1"), (2, "p1T_2")):
                    wait(pe, reader, t)
                wait(pe, "h_ready", t + 1)
                wait(pe, "gate_ready", t + 1)
                wait(pe, "dT_ready", t + 1)
                m = mask[:, t, :].unsqueeze(1) if isinstance(t, int) else mask[:, bass.ds(t, 1), :]
                for q in range(3):
                    pe.matmul(ps_d[:, q, :].rearrange("p (a n) -> p a n", a=4), ident_100[:],
                              m.broadcast_to([P, 4, N]), start=True, stop=False)
                    for a in range(4 * q, 4 * q + 4):
                        last = pe.matmul(ps_d[:, q, (a % 4) * N:(a % 4 + 1) * N], pick_b[:, a, :], dT[:],
                                         start=False, stop=(a % 4 == 3))
                last.then_inc(S["logits_ready"], 1)

            def turn_p1(t, next_is_here):
                if next_is_here:
                    wait(pe, "h_ready", t + 2)
                    wait(pe, "gate_ready", t + 2)
                for q in range(3):
                    wait(pe, "exp1_ready", 3 * t + q + 1)
                    for a in range(4 * q, 4 * q + 4):
                        last = pe.transpose(ps_d[:, q, (a % 4) * N:(a % 4 + 1) * N], z[:, a, :], ident[:])
                    last.then_inc(S["p1_turned"], 1)

            def apply_p1(t, par2, next_is_here):
                if next_is_here:
                    wait(pe, "dT_ready", t + 2)
                for q in range(3):
                    wait(pe, f"p1T_{q}", t + 1)
                    for a in range(4 * q, 4 * q + 4):
                        last = pe.matmul(ps_c[:, a * E1:(a + 1) * E1], p1T[:, a, :], h[:, par2, a, :],
                                         start=True, stop=True)
                last.then_inc(S["ph_made"], 1)

            pe.wait_ge(S["ident_in_ready"], 16)
            pe.wait_ge(S["consts_ready"], 3)

            def iteration(g, par, n):
                qkv, att, gat = parts(n)
                if qkv:
                    turn_x(g)
                for j in range(G):
                    ta, tl = G * (g - 1) + j, G * (g - 2) + j
                    tail = has_tail(n, j)
                    if att:
                        if n == 1 and j == 0:
                            wait(pe, "mask_ready", 4)
                        scores(ta, g, 1 - par, j)
                    if gat:
                        turn_x1(tl, par, j)
                    if qkv:
                        fill(g, n, j, "a")
                    if gat:
                        project_h_gate(tl, n, j)
                    if att:
                        turn_p0(ta)
                    if gat:
                        turn_th(tl)
                    if qkv:
                        fill(g, n, j, "b")
                    if att:
                        context(ta, g, 1 - par, j, n)
                    if gat:
                        src_dst(tl, n, j)
                    if tail:
                        turn_p1(tl - 1, gat)
                    if gat:
                        turn_dst(tl)
                    if att:
                        project_out(ta, g, j, n)
                    if gat:
                        logits(tl)
                    if tail:
                        apply_p1(tl - 1, (j + 1) % 2, gat)
            pipeline(pe, iteration)

        @block_.scalar
        def _(act):
            act.dma_start(block[:], block_in).then_inc(S["const_in"], 16)
            act.dma_start(pick, pick_in).then_inc(S["const_in"], 16)
            for s, w in enumerate((w_src, w_dst)):
                act.dma_start(w_cols[:, s, :], w).then_inc(S["const_in"], 16)
            act.dma_start(bq_col[:], bq).then_inc(S["const_in"], 16)
            act.dma_start(bk_col[:], bk).then_inc(S["const_in"], 16)
            act.dma_start(bv_all[:], bv.partition_broadcast(P)).then_inc(S["const_in"], 16)
            act.dma_start(bf_all[:], bf.partition_broadcast(P)).then_inc(S["const_in"], 16)
            act.dma_start(b1_all[:], b1.partition_broadcast(P)).then_inc(S["const_in"], 16)
            act.dma_start(hb_row[:], Hb.rearrange("(o d) -> o d", o=1)).then_inc(S["const_in"], 16)
            act.wait_ge(S["bias_ready"], 1)

            def iteration(g, par, n):
                qkv, att, gat = parts(n)

                def evacuate_q(m, bank):
                    wait(act, "q_made", 3 * g + m + 1)
                    act.activation(qT[:, par, m, :], bank[:], ACT.Identity, bias=bq8[:, m:m + 1],
                                   scale=D0 ** -0.5).then_inc(S["q_ready"], 1)

                def evacuate_k(m, bank):
                    wait(act, "k_made", 3 * g + m + 1)
                    act.activation(kT[:, par, m, :], bank[:], ACT.Identity,
                                   bias=bk_col[:, m:m + 1]).then_inc(S["k_ready"], 1)

                def exp1(t, q):
                    if q == 0:
                        wait(act, "leaky_ready", t + 1)
                        wait(act, "neg1_ready", t + 1)
                    for a in range(4 * q, 4 * q + 4):
                        last = act.activation(z[:, a, :], z[:, a, :], ACT.Exp, bias=neg1[:, a:a + 1])
                    last.then_inc(S["exp1_ready"], 1)

                if qkv:
                    for j in range(G):
                        wait(act, "x_turned", G * g + j + 1)
                        act.activation(xT[0][:, :, j * N:(j + 1) * N],
                                       (ps_a, ps_b)[j % 2][:, 0:D].rearrange("p (c n) -> p c n", c=C),
                                       ACT.Copy).then_inc(S["x_hi"], 1)
                for j in range(G):
                    ta, tl = G * (g - 1) + j, G * (g - 2) + j
                    tail = has_tail(n, j)
                    if gat:
                        wait(act, "x1_turned", tl + 1)
                        act.activation(x1T[0][:], ps_c[:, 0:D].rearrange("p (c n) -> p c n", c=C),
                                       ACT.Copy).then_inc(S["x1_hi"], 1)
                    if att:
                        wait(act, "neg_ready", ta + 1)
                        wait(act, "p0_turned", ta)
                        for o in range(2):
                            for i in range(C):
                                k = C * o + i
                                last = act.activation(p0[:, o, i, :], ps_s[:, o, i * N:(i + 1) * N], ACT.Exp,
                                                      bias=neg0[:, k:k + 1], accum_out=sum0[:, k:k + 1])
                        last.then_inc(S["exp0_ready"], 1)
                    if qkv and j == 0:
                        evacuate_q(0, ps_a)
                    elif qkv and j == 1:
                        evacuate_q(2, ps_a)
                    elif qkv and j == 2:
                        evacuate_k(1, ps_a)
                    if has_tail(n, j, 2):
                        wait(act, "fm_ready", tl - 1)
                        act.activation(fe[:], fe[:], ACT.Exp).then_inc(S["fe_ready"], 1)
                    if tail:
                        exp1(tl - 1, 0)
                    if gat:
                        wait(act, "h_made", tl + 1)
                        wait(act, "th_turned", tl)
                        act.activation(th[:], ps_d[:, 1, 0:D], ACT.Tanh).then_inc(S["th_ready"], 1)
                        wait(act, "gate_made", tl + 1)
                        wait(act, "r1_ready", tl - 1)
                        act.activation(gate[:, j % 2, :], ps_d[:, 2, 0:D], ACT.Tanh,
                                       scale=0.5).then_inc(S["gate_ready"], 1)
                    if att:
                        wait(act, "p0_turned", ta + 1)
                        wait(act, "ctx_made", ta)
                        act.activation(p0T[:, 0, :, :], ps_s[:, 0, 0:C * N].rearrange("p (i n) -> p i n", i=C),
                                       ACT.Copy).then_inc(S["p0T_even"], 1)
                    if gat:
                        wait(act, "th_turned", tl + 1)
                        wait(act, "sd_made", tl)
                        act.activation(thT[:], ps_c[:, 0:D].rearrange("p (c n) -> p c n", c=C),
                                       ACT.Copy).then_inc(S["thT_ready"], 1)
                    if tail:
                        exp1(tl - 1, 1)
                    if qkv and j == 0:
                        evacuate_q(1, ps_b)
                    elif qkv and j == 1:
                        evacuate_k(0, ps_b)
                    elif qkv and j == 2:
                        evacuate_k(2, ps_b)
                    if tail:
                        exp1(tl - 1, 2)
                    if att:
                        wait(act, "ctx_made", ta + 1)
                        wait(act, "out_made", ta)
                        act.activation(ctxT[0][:], ps_a[:, 0:D].rearrange("p (c n) -> p c n", c=C),
                                       ACT.Copy).then_inc(S["ctx_hi"], 1)
                    if tail:
                        wait(act, "p1_turned", 3 * (tl - 1) + 1)
                        wait(act, "ph_made", tl - 1)
                        act.activation(p1T[:, 0:4, :], ps_d[:, 0, :].rearrange("p (a n) -> p a n", a=4),
                                       ACT.Copy).then_inc(S["p1T_0"], 1)
                    if gat:
                        wait(act, "d_turned", tl + 1)
                        wait(act, "logits_ready", tl)
                        act.activation(dT[:], ps_c[0:3 * H1, 0:N // 2].bitcast(BF16), ACT.Copy).then_inc(S["dT_ready"], 1)
            pipeline(act, iteration)

        @block_.vector
        def _(dve):
            dve.wait_ge(S["ident_in_ready"], 16)
            dve.wait_ge(S["const_in"], 16 * 10)
            dve.tensor_copy(ident_b[:], ident[:]).then_inc(S["consts_ready"], 1)
            dve.tensor_scalar(ident_53[:], ident[:], 2.0 ** 53, None, ALU.mult).then_inc(S["consts_ready"], 1)
            dve.tensor_scalar(ident_100[:], ident[:], 2.0 ** 100, None, ALU.mult).then_inc(S["consts_ready"], 1)
            dve.tensor_scalar(bq8[:], bq_col[:], D0 ** -0.5, None, ALU.mult).then_inc(S["bias_ready"], 1)
            for n, name in enumerate(W_ORDER):
                hi, lo = w_parts[name]
                dve.wait_ge(S[f"weight_in_{n % 2}"], 16 * C * (n // 2 + 1))
                dve.tensor_copy(hi[:], stage[n % 2]).then_inc(S["weight_hi"], 1)
                dve.wait_ge(S["weight_hi"], n + 1)
                dve.tensor_tensor(lo[:], stage[n % 2], hi[:].bitcast(F32), ALU.subtract).then_inc(S["weight_lo"], 1)
            dve.wait_ge(S["weight_lo"], len(W_ORDER))

            def iteration(g, par, n):
                qkv, att, gat = parts(n)

                def lo_part(parts_, source, at, name_hi, count, name_lo):
                    wait(dve, name_hi, count)
                    dve.tensor_tensor(parts_[1][:, :, at], source[:, 0:D].rearrange("p (c n) -> p c n", c=C),
                                      parts_[0][:, :, at].bitcast(F32), ALU.subtract).then_inc(S[name_lo], 1)

                def evacuate_v(j, bank):
                    wait(dve, "v_made", G * g + j + 1)
                    dve.tensor_tensor(v[:, par, j, :], bank[:, 0:D], bv_all[:], ALU.add).then_inc(S["v_ready"], 1)

                if qkv:
                    for j in range(G):
                        lo_part(xT, (ps_a, ps_b)[j % 2], slice(j * N, (j + 1) * N), "x_hi", G * g + j + 1, "x_lo")
                for j in range(G):
                    ta, tl = G * (g - 1) + j, G * (g - 2) + j
                    tt = tl - 1
                    tail = has_tail(n, j)
                    if att:
                        wait(dve, "scores_ready", ta + 1)
                        dve.tensor_reduce(max0.rearrange("p (o i) -> p o i", o=2),
                                          ps_s[:, :, 0:C * N].rearrange("p o (i n) -> p o i n", i=C),
                                          AX_X, ALU.max).then_inc(S["att_small"], 1)
                        wait(dve, "att_small", ta + 1)
                        wait(dve, "exp0_ready", ta)
                        dve.tensor_scalar(neg0, max0, -1.0, None, ALU.mult).then_inc(S["neg_ready"], 1)
                    if gat:
                        lo_part(x1T, ps_c, slice(0, N), "x1_hi", tl + 1, "x1_lo")
                    if qkv and j == 3:
                        for b in (0, 1):
                            evacuate_v(b, (ps_a, ps_b)[b])
                    if tail:
                        wait(dve, "z_ready", tt + 1)
                        dve.scalar_tensor_tensor(z[:], z[:], 0.2, z[:], ALU.mult, ALU.max
                                                 ).then_inc(S["leaky_ready"], 1)
                        src_ = sd[:, (j + 1) % 2, 0, :]
                        wait(dve, "dmax_ready", tt + 1)
                        dve.tensor_tensor(zmax, dmax, src_, ALU.add).then_inc(S["max1_small"], 1)
                        wait(dve, "max1_small", 2 * tt + 1)
                        dve.scalar_tensor_tensor(m1, zmax, 0.2, zmax, ALU.mult, ALU.max).then_inc(S["max1_small"], 1)
                        wait(dve, "max1_small", 2 * tt + 2)
                        wait(dve, "exp1_ready", 3 * tt)
                        dve.tensor_scalar(neg1, m1, -1.0, None, ALU.mult).then_inc(S["neg1_ready"], 1)
                    if att:
                        wait(dve, "exp0_ready", ta + 1)
                        wait(dve, "p0_ready", ta)
                        dve.reciprocal(inv0, sum0).then_inc(S["inv0_ready"], 1)
                    if has_tail(n, j, 2):
                        t2 = tl - 2
                        flat = lambda w: w[:].rearrange("p a e -> p (a e)")
                        x1_ = x1[:, par if j > 1 else 1 - par, (j - 2) % G, :]
                        wait(dve, "fe_ready", t2 + 1)
                        wait(dve, "y_ready", t2)
                        dve.scalar_tensor_tensor(r1[:], flat(f), 0.0, flat(fe), ALU.max, ALU.add
                                                 ).then_inc(S["tail_small"], 1)
                        wait(dve, "tail_small", 3 * t2 + 1)
                        dve.scalar_tensor_tensor(r1[:], r1[:], -1.0, x1_, ALU.add, ALU.subtract
                                                 ).then_inc(S["tail_small"], 1)
                        wait(dve, "tail_small", 3 * t2 + 2)
                        dve.scalar_tensor_tensor(r1[:], gate[:, j % 2, :], 1.0, r1[:], ALU.add, ALU.mult
                                                 ).then_inc(S["tail_small"], 1)
                        wait(dve, "tail_small", 3 * t2 + 3)
                        dve.scalar_tensor_tensor(r1[:], r1[:], 0.25, x1_, ALU.mult, ALU.add).then_inc(S["r1_ready"], 1)
                        wait(dve, "r1_ready", t2 + 1)
                        dve.bn_stats(st1, r1[:]).then_inc(S["mv1_ready"], 1)
                        wait_apart(dve, "mv1_ready", 2 * t2 + 1)
                        dve.bn_aggr(mv1, st1).then_inc(S["mv1_ready"], 1)
                    if gat:
                        wait(dve, "th_ready", tl + 1)
                        wait(dve, "ph_made", tl - 1)
                        dve.tensor_copy(h[:, j % 2, :, 0:D1], ps_d[:, 1, 0:D].rearrange("p (a e) -> p a e", a=H1)
                                        ).then_inc(S["h_ready"], 1)
                    if att:
                        wait(dve, "p0_turned", ta + 1)
                        wait(dve, "ctx_made", ta)
                        dve.tensor_copy(p0T[:, 1, :, :], ps_s[:, 1, 0:C * N].rearrange("p (i n) -> p i n", i=C)
                                        ).then_inc(S["p0T_odd"], 1)
                    if qkv and j == 3:
                        for b in (2, 3):
                            evacuate_v(b, (ps_a, ps_b)[b % 2])
                    if att:
                        wait(dve, "ctx_made", ta + 1)
                        lo_part(ctxT, ps_a, slice(0, N), "ctx_hi", ta + 1, "ctx_lo")
                    if gat:
                        wait(dve, "sd_made", tl + 1)
                        wait(dve, "dst3_ready", tl - 1)
                        dve.tensor_copy(sd[:, j % 2, :, :], ps_c[:, 0:2 * H1].rearrange("p (s a) -> p s a", s=2)
                                        ).then_inc(S["sd_ready"], 1)
                    if tail:
                        for q in (1, 2):
                            wait(dve, "p1_turned", 3 * tt + q + 1)
                            wait(dve, "ph_made", tt)
                            dve.tensor_copy(p1T[:, 4 * q:4 * q + 4, :],
                                            ps_d[:, q, :].rearrange("p (a n) -> p a n", a=4)
                                            ).then_inc(S[f"p1T_{q}"], 1)
                    if att:
                        wait(dve, "out_made", ta + 1)
                        wait(dve, "xb_ready", ta + 1)
                        wait(dve, "x1_ready", ta)
                        dve.tensor_tensor(r0[:], ps_b[:, 0:D], xb[:, 1 - par, j, :], ALU.add).then_inc(S["r0_ready"], 1)
                        wait(dve, "r0_ready", ta + 1)
                        dve.bn_stats(st0, r0[:]).then_inc(S["mv0_ready"], 1)
                        wait_apart(dve, "mv0_ready", 2 * ta + 1)
                        dve.bn_aggr(mv0, st0).then_inc(S["mv0_ready"], 1)
                    if gat:
                        src = sd[:, j % 2, 0, :]
                        wait(dve, "logits_ready", tl + 1)
                        dve.tensor_reduce(dmax, ps_d[:, :, :].rearrange("p q (a n) -> p (q a) n", a=4), AX_X, ALU.max
                                          ).then_inc(S["dmax_ready"], 1)
                        wait(dve, "p1_turned", 3 * tl)
                        dve.tensor_tensor(z[:], ps_d[:, :, :].rearrange("p q (a n) -> p (q a) n", a=4),
                                          src.unsqueeze(2).broadcast_to([P, H1, N]), ALU.add).then_inc(S["z_ready"], 1)
                    if tail:
                        ph = ps_c[:, 0:H1 * E1].rearrange("p (a e) -> p a e", a=H1)
                        wait(dve, "ph_made", tt + 1)
                        dve.reciprocal(inv1.unsqueeze(2), ph[:, :, D1:E1]).then_inc(S["inv1_ready"], 1)
                        wait(dve, "inv1_ready", tt + 1)
                        wait(dve, "tail_small", 3 * (tt - 1) + 1)
                        dve.tensor_tensor(f[:], ph[:, :, 0:D1], inv1.unsqueeze(2).broadcast_to([P, H1, D1]),
                                          ALU.mult).then_inc(S["f0_ready"], 1)
            pipeline(dve, iteration)

        @block_.gpsimd
        def _(pool):
            pool.memset(minus_half[:], -0.5)
            pool.memset(ones_b[:], 1.0)
            for k in range(2):
                pool.memset(h[:, k, :, D1:E1], 1.0)
            for s in range(4):
                wait(pool, "mask_ready", s)
                pool.dma_start(adj_u8, adj_dram[s]).then_inc(S["adj_in"], 16)
                pool.wait_ge(S["adj_in"], 16 * (s + 1))
                pool.tensor_scalar(mask[:, 16 * s:16 * s + 16, :], adj_u8, 1.0, -1.0, ALU.mult, ALU.add
                                   ).then_inc(S["mask_ready"], 1)
            pool.wait_ge(S["const_in"], 16 * 10)
            pool.tensor_copy(pick_b[:], pick).then_inc(S["pick_ready"], 1)
            for s in range(2):
                pool.tensor_tensor(w_sd[:, :, s, :], block[:], w_cols[:, s, :].unsqueeze(2).broadcast_to([P, C, H1]),
                                   ALU.mult).then_inc(S["wsd_ready"], 1)
            pool.tensor_copy(hb_split[:, 0, :], hb_row[:]).then_inc(S["split_small"], 1)
            pool.wait_ge(S["split_small"], 1)
            pool.tensor_tensor(hb_rest[:, 0, :], hb_row[:], hb_split[:, 0, :], ALU.subtract).then_inc(S["split_small"], 1)
            pool.wait_ge(S["split_small"], 2)
            pool.tensor_copy(hb_split[:, 1, :], hb_rest[:, 0, :]).then_inc(S["split_small"], 1)
            pool.wait_ge(S["split_small"], 3)
            pool.tensor_tensor(hb_rest[:, 1, :], hb_rest[:, 0, :], hb_split[:, 1, :], ALU.subtract
                               ).then_inc(S["split_small"], 1)
            pool.wait_ge(S["split_small"], 4)
            pool.tensor_copy(hb_split[:, 2, :], hb_rest[:, 1, :]).then_inc(S["split_small"], 1)
            pool.wait_ge(S["split_small"], 5)
            pool.dma_start(hb_rows[:], hb_split[:]).then_inc(S["hb_moved"], 16)

            def normalise(r, mv, ve, rs, nm, eps, out_ap, small, count, done, ready):
                pool.tensor_scalar(ve, mv[:, 1:2], eps, None, ALU.add).then_inc(S[small], 1)
                wait(pool, small, count + 1)
                pool.tensor_tensor(rs, ve, minus_half[:], ALU.pow).then_inc(S[small], 1)
                wait_apart(pool, small, count + 2)
                pool.tensor_scalar(nm, mv[:, 0:1], -1.0, None, ALU.mult).then_inc(S[small], 1)
                wait_apart(pool, small, count + 3)
                pool.tensor_scalar(out_ap, r, nm, rs, ALU.add, ALU.mult).then_inc(S[ready], 1)

            def iteration(g, par, n):
                qkv, att, gat = parts(n)
                for j in range(G):
                    ta, tl = G * (g - 1) + j, G * (g - 2) + j
                    tt = tl - 1
                    tail = has_tail(n, j)
                    if att:
                        wait(pool, "inv0_ready", ta + 1)
                        pool.tensor_tensor(p0[:].rearrange("p o i n -> p (o i) n"),
                                           p0[:].rearrange("p o i n -> p (o i) n"),
                                           inv0.unsqueeze(2).broadcast_to([P, H0, N]), ALU.mult
                                           ).then_inc(S["p0_ready"], 1)
                    if qkv and j < 2:
                        for b in (2 * j, 2 * j + 1):
                            wait(pool, "x_in_ready", 16 * (g + 1))
                            wait(pool, "r0_ready", G * (g - 2) + b + 1)
                            pool.tensor_tensor(xb[:, par, b, :], x_in[:, b, :], bf_all[:], ALU.add
                                               ).then_inc(S["xb_ready"], 1)
                    if has_tail(n, j, 2):
                        t2 = tl - 2
                        wait_apart(pool, "mv1_ready", 2 * t2 + 2)
                        wait_apart(pool, f"y_stored_{j % 2}", 16 * (2 * (g - 2) + (j - 2) // 2))
                        normalise(r1[:], mv1, ve1, rs1, nm1, EPS / 4, y[:, j % 2, :], "ln1_small", 3 * t2, None,
                                  "y_ready")
                    if gat:
                        dst = sd[:, j % 2, 1, :]
                        base = 5 + 4 * tl
                        wait_apart(pool, "sd_ready", tl + 1)
                        wait_apart(pool, "d_turned", tl)
                        pool.tensor_copy(dst3[:, 0, :], dst).then_inc(S["split_small"], 1)
                        wait(pool, "split_small", base + 1)
                        pool.tensor_tensor(dst_rest[:, 0, :], dst, dst3[:, 0, :], ALU.subtract).then_inc(S["split_small"], 1)
                        wait_apart(pool, "split_small", base + 2)
                        pool.tensor_copy(dst3[:, 1, :], dst_rest[:, 0, :]).then_inc(S["split_small"], 1)
                        wait(pool, "split_small", base + 3)
                        pool.tensor_tensor(dst_rest[:, 1, :], dst_rest[:, 0, :], dst3[:, 1, :], ALU.subtract
                                           ).then_inc(S["split_small"], 1)
                        wait_apart(pool, "split_small", base + 4)
                        pool.tensor_copy(dst3[:, 2, :], dst_rest[:, 1, :]).then_inc(S["dst3_ready"], 1)
                    if att:
                        wait_apart(pool, "mv0_ready", 2 * ta + 2)
                        wait_apart(pool, "r1_ready", ta - 7)
                        normalise(r0[:], mv0, ve0, rs0, nm0, EPS, x1[:, 1 - par, j, :], "ln0_small", 3 * ta, None,
                                  "x1_ready")
                    if tail:
                        wait(pool, "f0_ready", tt + 1)
                        pool.tensor_tensor(f[:], f[:], b1_all[:].unsqueeze(1).broadcast_to([P, H1, D1]), ALU.add
                                           ).then_inc(S["f1_ready"], 1)
                        wait_apart(pool, "f1_ready", tt + 1)
                        wait_apart(pool, "tail_small", 3 * (tt - 1) + 1)
                        pool.tensor_scalar(fe[:], f[:], 0.0, None, ALU.min).then_inc(S["fm_ready"], 1)
            pipeline(pool, iteration)


def kernel(**inputs):
    import numpy as _np
    import concourse.bacc as _bacc
    from concourse import mybir as _mybir
    from concourse.bass_utils import run_bass_kernel_spmd as _run

    nc = _bacc.Bacc("TRN2", target_bir_lowering=False, num_devices=1)
    names = ["x", "adj"] + ["L0_gnn_" + n for n in ("Wq", "bq", "Wk", "bk", "Wv", "bv", "Wf", "bf")] + [
        "L1_gnn_" + n for n in ("W", "b", "w_src", "w_dst", "H_w", "H_b")]
    held = {n: _np.asarray(inputs[n]) for n in names}
    held["L1_gnn_H_w"] = held["L1_gnn_H_w"].T
    for n in ("L0_gnn_bq", "L0_gnn_bk", "L1_gnn_w_src", "L1_gnn_w_dst"):
        held[n] = held[n].reshape(C, P).T
    held["ident"] = _np.eye(P, dtype=_np.float32)
    feature = _np.arange(P)[:, None, None] + P * _np.arange(C)[None, :, None]
    held["block"] = (feature // D1 == _np.arange(H1)[None, None, :]).astype(_np.float32)
    row = _np.arange(3 * H1)[:, None, None] % H1
    held["pick"] = _np.broadcast_to(row == _np.arange(H1)[None, :, None], (3 * H1, H1, P)).astype(_np.float32)
    arrays, args = {}, []
    for name, a in held.items():
        a = _np.ascontiguousarray(a)
        arrays[f"in_{name}_dram"] = a
        args.append(nc.dram_tensor(f"in_{name}_dram", a.shape, _mybir.dt.from_np(a.dtype), kind="ExternalInput").ap())
    out = nc.dram_tensor("out_0_dram", (B, N, D), F32, kind="ExternalOutput").ap()
    build_program(nc, *args, out)
    r = _run(nc, [arrays], core_ids=[0])
    return r.results[0]["out_0_dram"]
```

```python
from contextlib import ExitStack

import concourse.bass as bass
from concourse import mybir

ALU = mybir.AluOpType
ACT = mybir.ActivationFunctionType
F32 = mybir.dt.float32
F32R = mybir.dt.float32r
BF16 = mybir.dt.bfloat16
AX_X = mybir.AxisListType.X

B, N, D = 64, 128, 384
P = 128
C = D // P
G = 4
NG = B // G
H0, D0 = 6, 64
H1, D1 = 12, 32
E1 = D1 + 1
EPS = 1e-5
HI_LO = ((0, 0), (1, 0), (0, 1))


def build_program(nc, xT_in, x, adj, Wq, bq, Wk, bk, Wv, bv, Wf, bf, W1, b1, w_src, w_dst, HwT, Hb,
                  ident_in, pick_in, out):
    with ExitStack() as ctx:
        def sb(name, shape, dt=F32):
            return ctx.enter_context(nc.sbuf_tensor(name, shape, dt))

        def psum(name, shape, dt=F32):
            return ctx.enter_context(nc.psum_tensor(name, shape, dt))

        def sem(name):
            return ctx.enter_context(nc.semaphore(name))

        ps_a = psum("ps_a", [P, 512])
        ps_b = psum("ps_b", [P, 512])
        ps_s = psum("ps_s", [P, 2, 512])
        ps_c = psum("ps_c", [P, 512])
        ps_d = psum("ps_d", [P, 3, 512])

        ident = sb("ident", [P, P])
        ident_b = sb("ident_b", [P, P], BF16)
        ident_53 = sb("ident_53", [P, P], BF16)
        ident_100 = sb("ident_100", [P, P], BF16)
        pick_b = sb("pick_b", [3 * H1, H1, P], BF16)
        ones_b = sb("ones_b", [3, P], BF16)
        minus_half = sb("minus_half", [P, 1])
        w_parts = {n: [sb(f"{n}_hi", [P, C, D], F32R), sb(f"{n}_lo", [P, C, D], F32R)]
                   for n in ("wq", "wk", "wv", "wf", "w1", "hw")}
        bq_col = sb("bq_col", [P, C])
        bq8 = sb("bq8", [P, C])
        bk_col = sb("bk_col", [P, C])
        bv_all = sb("bv_all", [P, D])
        bf_all = sb("bf_all", [P, D])
        b1_all = sb("b1_all", [P, D1])
        w_sd = sb("w_sd", [P, 2, D])
        hb_rows = sb("hb_rows", [3, D], BF16)
        mask = sb("mask", [P, B, N], BF16)

        x_cols = sb("x_cols", [P, C, G * N])
        xT = [sb("xT_hi", [P, C, G * N], F32R), sb("xT_lo", [P, C, G * N], F32R)]
        xb = sb("xb", [P, 2, G, D])
        qT = sb("qT", [P, 2, C, G * N])
        kT = sb("kT", [P, 2, C, G * N])
        v = sb("v", [P, 2, G, D])
        p0 = sb("p0", [P, 2, C, N])
        p0T = sb("p0T", [P, 2, C, N])
        ctxT = [sb("ctxT_hi", [P, C, N], F32R), sb("ctxT_lo", [P, C, N], F32R)]
        r0 = sb("r0", [P, D])
        s0 = sb("s0", [P, 64])
        max0, neg0, sum0, inv0 = (s0[:, 8 * k:8 * k + H0] for k in range(4))
        st0, mv0, ve0, rs0, nm0 = s0[:, 32:38], s0[:, 40:42], s0[:, 44:45], s0[:, 46:47], s0[:, 48:49]
        x1 = sb("x1", [P, 2, G, D])
        x1T = [sb("x1T_hi", [P, C, N], F32R), sb("x1T_lo", [P, C, N], F32R)]
        h = sb("h", [P, 2, H1, E1])
        th = sb("th", [P, D])
        gate = sb("gate", [P, 2, D])
        thw = sb("thw", [P, 2, D])
        sd = sb("sd", [P, 2, 2, H1])
        dst_rest = sb("dst_rest", [P, 2, H1])
        dst3 = sb("dst3", [P, 3, H1], BF16)
        dT = sb("dT", [3 * H1, N], BF16)
        z = sb("z", [P, H1, N])
        s1 = sb("s1", [P, 64])
        dmax, zmax, m1, neg1 = (s1[:, 12 * k:12 * k + H1] for k in range(4))
        p1T = sb("p1T", [P, H1, N])
        s2 = sb("s2", [P, 64])
        inv1 = s2[:, 0:12]
        st1, mv1, ve1, rs1, nm1 = s2[:, 16:22], s2[:, 24:26], s2[:, 28:29], s2[:, 30:31], s2[:, 32:33]
        f = sb("f", [P, H1, D1])
        fe = sb("fe", [P, H1, D1])
        r1 = sb("r1", [P, D])
        y = sb("y", [P, 2, D])
        stage = [z[:, :, :].rearrange("p a n -> p (a n)")[:, 0:C * D].rearrange("p (c n) -> p c n", c=C),
                 p1T[:, :, :].rearrange("p a n -> p (a n)")[:, 0:C * D].rearrange("p (c n) -> p c n", c=C)]
        x1_flat = x1[:].rearrange("p a j d -> p (a j d)")
        pick = x1_flat[0:3 * H1, 0:H1 * P].rearrange("p (a n) -> p a n", a=H1)
        hb_row = r1[0:1, :]
        hb_rest = y[0:1, :, :]
        hb_split = gate[0:1, :, :].rearrange("p a d -> p (a d)").bitcast(BF16)[:, 0:3 * D].rearrange("p (a d) -> p a d", a=3)
        adj_u8 = x1_flat[:, 1536:1536 + B * N // 16].bitcast(mybir.dt.uint8).rearrange("p (b n) -> p b n", n=N)

        names = """ident_in_ready const_in weight_in_0 weight_in_1 adj_in x_in_ready weight_hi weight_lo mask_ready consts_ready pick_ready hb_moved
            bias_in bias_ready hb_small x_hi x_lo xb_in xb_ready q_made q_ready k_made k_ready v_made v_ready
            scores_ready att_small neg_ready exp0_ready inv0_ready p0_ready p0_turned p0T_even p0T_odd
            ctx_made ctx_hi ctx_lo out_made r0_ready mv0_ready ln0_small x1_ready
            x1_turned x1_hi x1_lo h_made h_ready th_ready gate_made gate_ready thw_ready
            sd_ready split_small dst3_ready d_turned dT_ready logits_ready dmax_ready z_ready max1_small neg1_ready
            leaky_ready exp1_ready p1_turned p1T_0 p1T_1 p1T_2 ph_made inv1_ready f0_ready f1_ready
            fm_ready fe_ready tail_small r1_ready mv1_ready ln1_small y_ready y_stored_0 y_stored_1"""
        S = {n: sem(n) for n in names.split()}

        def due(value):
            return not isinstance(value, int) or value > 0

        def apart(eng, value):
            if not isinstance(value, int):
                value = eng.to_reg(value)
                eng.wait_ge(S["ident_in_ready"], 16)
            return value

        W_ORDER = ["wq", "wk", "wv", "wf", "w1", "hw"]
        DRAM_W = {"wq": Wq, "wk": Wk, "wv": Wv, "wf": Wf, "hw": HwT}
        x_dram = x.rearrange("(g b) n d -> g n b d", b=G)
        adj_dram = adj.rearrange("(s b) n m -> s n b m", b=B // 4)
        out_dram = out

        def pipeline(eng, iteration):
            for g in (0, 1, 2):
                iteration(g, g % 2, g)
            with eng.Fori(0, (NG - 4) // 2) as pair:
                iteration(pair * 2 + 3, 1, 3)
                iteration(pair * 2 + 4, 0, 4)
            for g in range(NG - 1, NG + 3):
                iteration(g, g % 2, g)

        def parts(n):
            return n < NG, 1 <= n <= NG, 2 <= n <= NG + 1

        def has_tail(n, j, lag=1):
            return 0 <= G * (n - 2) + j - lag < B

        block_ = ctx.enter_context(nc.Block())

        @block_.sync
        def _(sp):
            sp.dma_start(x_cols[:], xT_in[0]).then_inc(S["x_in_ready"], 16)
            for n, name in enumerate(W_ORDER):
                if due(n - 1):
                    sp.wait_ge(S["weight_hi"], n - 1)
                if due(n - 1):
                    sp.wait_ge(S["weight_lo"], n - 1)
                if name == "w1":
                    for c in range(C):
                        sp.dma_start(stage[n % 2][:, c, :].rearrange("p (a e) -> p a e", a=H1),
                                     W1[:, c * P:(c + 1) * P, :].rearrange("a p e -> p a e")
                                     ).then_inc(S[f"weight_in_{n % 2}"], 16)
                else:
                    for c in range(C):
                        sp.dma_start(stage[n % 2][:, c, :],
                                     DRAM_W[name][c * P:(c + 1) * P, :]).then_inc(S[f"weight_in_{n % 2}"], 16)
                if n == 0:
                    sp.dma_start(ident[:], ident_in).then_inc(S["ident_in_ready"], 16)

            def iteration(g, par, n):
                qkv, att, gat = parts(n)
                if qkv:
                    if due(G * (g - 1)):
                        sp.wait_ge(S["r0_ready"], G * (g - 1))
                    if due(2 * g):
                        sp.wait_ge(S["xb_ready"], 2 * g)
                    sp.dma_start(xb[:, par, :, :], x_dram[g] if isinstance(g, int)
                                 else x_dram[bass.ds(g, 1)].rearrange("o n b d -> (o n) b d")
                                 ).then_inc(S["xb_in"], 16)
                if n + 1 < NG:
                    sp.wait_ge(S["x_lo"], 2 * (g + 1))
                    sp.dma_start(x_cols[:], xT_in[g + 1] if isinstance(g, int)
                                 else xT_in[bass.ds(g + 1, 1)].rearrange("o p c n -> (o p) c n")
                                 ).then_inc(S["x_in_ready"], 16)
                for j in range(G):
                    if has_tail(n, j, 2):
                        t = G * (g - 2) + j - 2
                        sp.wait_ge(S["y_ready"], t + 1)
                        dst = out_dram[t] if isinstance(t, int) else out_dram[bass.ds(t, 1)].rearrange("o n d -> (o n) d")
                        sp.dma_start(dst, y[:, j % 2, :]).then_inc(S[f"y_stored_{j % 2}"], 16)
            pipeline(sp, iteration)
            for k in range(2):
                sp.wait_ge(S[f"y_stored_{k}"], 16 * B // 2)

        @block_.tensor
        def _(pe):
            def split_product(out_ap, lhs, rhs, chunks=range(C)):
                for c in chunks:
                    for k, (a, b) in enumerate(HI_LO):
                        last = pe.matmul(out_ap, lhs(a, c), rhs(b, c), start=(c == 0 and k == 0),
                                         stop=(c == C - 1 and k == 2))
                return last

            def project_qk(name, m, bank, chunks=range(C)):
                last = split_product(bank[:], lambda a, c: w_parts[name][a][:, c, m * P:(m + 1) * P],
                                     lambda b, c: xT[b][:, c, :], chunks)
                if chunks[-1] == C - 1:
                    last.then_inc(S["q_made" if name == "wq" else "k_made"], 1)

            def project_v(j, bank):
                split_product(bank[:, 0:D], lambda a, c: xT[a][:, c, j * N:(j + 1) * N],
                              lambda b, c: w_parts["wv"][b][:, c, :]).then_inc(S["v_made"], 1)

            def fill_a(g, n, j):
                if j == 0:
                    pe.wait_ge(S["x_lo"], 2 * (g + 1))
                    if due(G * g):
                        pe.wait_ge(S["v_ready"], G * g)
                if parts(n)[1]:
                    if due(G * (g - 1) + j):
                        pe.wait_ge(S["ctx_lo"], G * (g - 1) + j)
                if j == 0:
                    if n == 0:
                        pe.wait_ge(S["weight_lo"], 1)
                    project_qk("wq", 0, ps_a)
                elif j == 1:
                    pe.wait_ge(S["q_ready"], 3 * g + 1)
                    project_qk("wq", 2, ps_a)
                elif j == 2:
                    pe.wait_ge(S["q_ready"], 3 * g + 3)
                    project_qk("wk", 1, ps_a)
                else:
                    if n == 0:
                        pe.wait_ge(S["weight_lo"], 3)
                    pe.wait_ge(S["k_ready"], 3 * g + 2)
                    project_v(0, ps_a)
                    if parts(n)[1]:
                        if due(G * (g - 1) + j):
                            pe.wait_ge(S["r0_ready"], G * (g - 1) + j)
                    pe.wait_ge(S["k_ready"], 3 * g + 3)
                    project_v(1, ps_b)

            def fill_b(g, n, j, half):
                chunks = (0, 1) if half == 0 else (2,)
                if j == 3:
                    pe.wait_ge(S["v_ready"], G * g + 1 + half)
                    project_v(2 + half, (ps_a, ps_b)[half])
                    return
                if half == 0:
                    if parts(n)[1]:
                        if due(G * (g - 1) + j):
                            pe.wait_ge(S["r0_ready"], G * (g - 1) + j)
                    if j == 1:
                        pe.wait_ge(S["q_ready"], 3 * g + 2)
                        if n == 0:
                            pe.wait_ge(S["weight_lo"], 2)
                    elif j == 2:
                        pe.wait_ge(S["k_ready"], 3 * g + 1)
                project_qk(*(("wq", 1), ("wk", 0), ("wk", 2))[j], ps_b, chunks)

            def scores(t, g, par, j):
                if due(t):
                    pe.wait_ge(S["p0T_even"], t)
                if due(t):
                    pe.wait_ge(S["p0T_odd"], t)
                if j == 0:
                    if due(3 * g):
                        pe.wait_ge(S["q_ready"], 3 * g)
                    if due(3 * g):
                        pe.wait_ge(S["k_ready"], 3 * g)
                m = mask[:, t, :].unsqueeze(1) if isinstance(t, int) else mask[:, bass.ds(t, 1), :]
                for o in range(2):
                    pe.matmul(ps_s[:, o, 0:C * N].rearrange("p (i n) -> p i n", i=C), ident_53[:],
                              m.broadcast_to([P, C, N]), start=True, stop=False)
                for i in range(C):
                    for o in range(2):
                        q_, k_ = (w[D0 * o:D0 * (o + 1), par, i, j * N:(j + 1) * N] for w in (qT, kT))
                        last = pe.matmul(ps_s[:, o, i * N:(i + 1) * N], q_, k_, start=False, stop=(i == C - 1))
                last.then_inc(S["scores_ready"], 1)

            def turn_p0(t):
                pe.wait_ge(S["p0_ready"], t + 1)
                for o in range(2):
                    for i in range(C):
                        last = pe.transpose(ps_s[:, o, i * N:(i + 1) * N], p0[:, o, i, :], ident[:])
                last.then_inc(S["p0_turned"], 1)

            def context(t, g, par, j, n):
                if j == 0:
                    if due(G * g):
                        pe.wait_ge(S["v_ready"], G * g)
                if parts(n)[0]:
                    if j < 2:
                        if due(3 * g + 2 * j + 1):
                            pe.wait_ge(S["q_ready"], 3 * g + 2 * j + 1)
                    elif j == 2:
                        pe.wait_ge(S["k_ready"], 3 * g + 2)
                    else:
                        pe.wait_ge(S["v_ready"], G * g + 3)
                else:
                    if due(t):
                        pe.wait_ge(S["ctx_lo"], t)
                pe.wait_ge(S["p0T_even"], t + 1)
                pe.wait_ge(S["p0T_odd"], t + 1)
                for o in range(2):
                    for i in range(C):
                        hd = 2 * i + o
                        last = pe.matmul(ps_a[D0 * o:D0 * (o + 1), i * N:(i + 1) * N],
                                         v[:, par, j, hd * D0:(hd + 1) * D0], p0T[:, o, i, :], start=True, stop=True)
                last.then_inc(S["ctx_made"], 1)

            def project_out(t, g, j, n):
                if parts(n)[0]:
                    if j == 0:
                        pe.wait_ge(S["q_ready"], 3 * g + 2)
                    elif j < 3:
                        if due(3 * g + 2 * j - 1):
                            pe.wait_ge(S["k_ready"], 3 * g + 2 * j - 1)
                    else:
                        pe.wait_ge(S["v_ready"], G * g + 4)
                else:
                    if due(t):
                        pe.wait_ge(S["r0_ready"], t)
                pe.wait_ge(S["ctx_lo"], t + 1)
                if n == 1 and j == 0:
                    pe.wait_ge(S["weight_lo"], 4)
                split_product(ps_b[:, 0:D], lambda a, c: ctxT[a][:, c, :],
                              lambda b, c: w_parts["wf"][b][:, c, :]).then_inc(S["out_made"], 1)

            def turn_x1(t, par, j):
                if due(t - 1):
                    pe.wait_ge(S["f0_ready"], t - 1)
                pe.wait_ge(S["x1_ready"], t + 1)
                for c in range(C):
                    last = pe.transpose(ps_c[:, c * P:(c + 1) * P], x1[:, par, j, c * P:(c + 1) * P], ident[:])
                last.then_inc(S["x1_turned"], 1)

            def project_h_gate(t, n, j):
                pe.wait_ge(S["x1_lo"], t + 1)
                if due(t):
                    pe.wait_ge(S["z_ready"], t)
                if n == 2 and j == 0:
                    pe.wait_ge(S["weight_lo"], 6)
                    pe.wait_ge(S["hb_moved"], 16)
                    pe.wait_ge(S["pick_ready"], 1)
                split_product(ps_d[:, 1, 0:D], lambda a, c: x1T[a][:, c, :],
                              lambda b, c: w_parts["w1"][b][:, c, :]).then_inc(S["h_made"], 1)
                for c in range(C):
                    for a, b in HI_LO:
                        pe.matmul(ps_d[:, 2, 0:D], x1T[a][:, c, :], w_parts["hw"][b][:, c, :],
                                  start=(c == 0 and (a, b) == HI_LO[0]), stop=False)
                pe.matmul(ps_d[:, 2, 0:D], ones_b[:], hb_rows[:], start=False, stop=True).then_inc(S["gate_made"], 1)

            def turn_dst(t):
                pe.wait_ge(S["dst3_ready"], apart(pe, t + 1))
                pe.transpose(ps_c[0:3 * H1, 0:N // 2].bitcast(BF16), dst3[:, :, :].rearrange("p s a -> p (s a)"),
                             ident_b[:]).then_inc(S["d_turned"], 1)

            def logits(t):
                for q in range(3):
                    if due(t):
                        pe.wait_ge(S[f"p1T_{q}"], t)
                pe.wait_ge(S["h_ready"], t + 1)
                pe.wait_ge(S["gate_ready"], t + 1)
                pe.wait_ge(S["dT_ready"], t + 1)
                m = mask[:, t, :].unsqueeze(1) if isinstance(t, int) else mask[:, bass.ds(t, 1), :]
                for q in range(3):
                    pe.matmul(ps_d[:, q, :].rearrange("p (a n) -> p a n", a=4), ident_100[:],
                              m.broadcast_to([P, 4, N]), start=True, stop=False)
                    for a in range(4 * q, 4 * q + 4):
                        last = pe.matmul(ps_d[:, q, (a % 4) * N:(a % 4 + 1) * N], pick_b[:, a, :], dT[:],
                                         start=False, stop=(a % 4 == 3))
                last.then_inc(S["logits_ready"], 1)

            def turn_p1(t, next_is_here):
                if next_is_here:
                    pe.wait_ge(S["h_ready"], t + 2)
                    pe.wait_ge(S["gate_ready"], t + 2)
                for q in range(3):
                    pe.wait_ge(S["exp1_ready"], 3 * t + q + 1)
                    for a in range(4 * q, 4 * q + 4):
                        last = pe.transpose(ps_d[:, q, (a % 4) * N:(a % 4 + 1) * N], z[:, a, :], ident[:])
                    last.then_inc(S["p1_turned"], 1)

            def apply_p1(t, par2, next_is_here):
                if next_is_here:
                    pe.wait_ge(S["dT_ready"], t + 2)
                for q in range(3):
                    pe.wait_ge(S[f"p1T_{q}"], t + 1)
                    for a in range(4 * q, 4 * q + 4):
                        last = pe.matmul(ps_c[:, a * E1:(a + 1) * E1], p1T[:, a, :], h[:, par2, a, :],
                                         start=True, stop=True)
                last.then_inc(S["ph_made"], 1)

            def iteration(g, par, n):
                qkv, att, gat = parts(n)
                for j in range(G):
                    ta, tl = G * (g - 1) + j, G * (g - 2) + j
                    tail = has_tail(n, j)
                    if att:
                        if n == 1 and j == 0:
                            pe.wait_ge(S["consts_ready"], 3)
                            pe.wait_ge(S["mask_ready"], 4)
                        scores(ta, g, 1 - par, j)
                    if gat:
                        turn_x1(tl, par, j)
                    if qkv:
                        fill_a(g, n, j)
                    if gat:
                        project_h_gate(tl, n, j)
                    if qkv:
                        fill_b(g, n, j, 0)
                    if att:
                        turn_p0(ta)
                    if qkv:
                        fill_b(g, n, j, 1)
                    if att:
                        context(ta, g, 1 - par, j, n)
                    if tail:
                        turn_p1(tl - 1, gat)
                    if gat:
                        turn_dst(tl)
                    if att:
                        project_out(ta, g, j, n)
                    if gat:
                        logits(tl)
                    if tail:
                        apply_p1(tl - 1, (j + 1) % 2, gat)
            pipeline(pe, iteration)

        @block_.scalar
        def _(act):
            act.dma_start(bq_col[:], bq).then_inc(S["bias_in"], 16)
            act.dma_start(bk_col[:], bk).then_inc(S["bias_in"], 16)
            act.dma_start(pick, pick_in).then_inc(S["const_in"], 16)
            for s, w in enumerate((w_src, w_dst)):
                act.dma_start(w_sd[:, s, :], w.partition_broadcast(P)).then_inc(S["const_in"], 16)
            act.dma_start(bv_all[:], bv.partition_broadcast(P)).then_inc(S["const_in"], 16)
            act.dma_start(bf_all[:], bf.partition_broadcast(P)).then_inc(S["const_in"], 16)
            act.dma_start(b1_all[:], b1.partition_broadcast(P)).then_inc(S["const_in"], 16)
            act.dma_start(hb_row, Hb.rearrange("(o d) -> o d", o=1)).then_inc(S["const_in"], 16)

            def x_hi(g, half):
                at = slice(2 * half * N, 2 * (half + 1) * N)
                act.wait_ge(S["x_in_ready"], 16 * (g + 1))
                if due(G * (g - 1) + 2 * (half + 1)):
                    act.wait_ge(S["v_made"], G * (g - 1) + 2 * (half + 1))
                act.activation(xT[0][:, :, at], x_cols[:, :, at], ACT.Copy).then_inc(S["x_hi"], 1)

            x_hi(0, 0)
            x_hi(0, 1)
            for n, name in enumerate(W_ORDER):
                act.wait_ge(S[f"weight_in_{n % 2}"], 16 * C * (n // 2 + 1))
                act.activation(w_parts[name][0][:], stage[n % 2], ACT.Copy).then_inc(S["weight_hi"], 1)
                if n == 1:
                    act.wait_ge(S["bias_ready"], 1)

            def iteration(g, par, n):
                qkv, att, gat = parts(n)

                def evacuate_q(m, bank):
                    act.wait_ge(S["q_made"], 3 * g + m + 1)
                    act.activation(qT[:, par, m, :], bank[:], ACT.Identity, bias=bq8[:, m:m + 1],
                                   scale=D0 ** -0.5).then_inc(S["q_ready"], 1)

                def evacuate_k(m, bank):
                    act.wait_ge(S["k_made"], 3 * g + m + 1)
                    act.activation(kT[:, par, m, :], bank[:], ACT.Identity,
                                   bias=bk_col[:, m:m + 1]).then_inc(S["k_ready"], 1)

                def exp1(t, q):
                    if q == 0:
                        act.wait_ge(S["leaky_ready"], t + 1)
                        act.wait_ge(S["neg1_ready"], t + 1)
                    for a in range(4 * q, 4 * q + 4):
                        last = act.activation(z[:, a, :], z[:, a, :], ACT.Exp, bias=neg1[:, a:a + 1])
                    last.then_inc(S["exp1_ready"], 1)

                def turned_p1(t, q):
                    act.wait_ge(S["p1_turned"], 3 * t + q + 1)
                    if due(t):
                        act.wait_ge(S["ph_made"], t)
                    act.activation(p1T[:, 4 * q:4 * q + 4, :], ps_d[:, q, :].rearrange("p (a n) -> p a n", a=4),
                                   ACT.Copy).then_inc(S[f"p1T_{q}"], 1)

                for j in range(G):
                    ta, tl = G * (g - 1) + j, G * (g - 2) + j
                    tail = has_tail(n, j)
                    if gat:
                        act.wait_ge(S["x1_turned"], tl + 1)
                        act.activation(x1T[0][:], ps_c[:, 0:D].rearrange("p (c n) -> p c n", c=C),
                                       ACT.Copy).then_inc(S["x1_hi"], 1)
                    if att:
                        act.wait_ge(S["neg_ready"], ta + 1)
                        if due(ta):
                            act.wait_ge(S["p0_turned"], ta)
                        for o in range(2):
                            for i in range(C):
                                k = C * o + i
                                last = act.activation(p0[:, o, i, :], ps_s[:, o, i * N:(i + 1) * N], ACT.Exp,
                                                      bias=neg0[:, k:k + 1], accum_out=sum0[:, k:k + 1])
                        last.then_inc(S["exp0_ready"], 1)
                    if qkv and j == 0:
                        evacuate_q(0, ps_a)
                    elif qkv and j == 1:
                        evacuate_q(2, ps_a)
                    elif qkv and j == 2:
                        evacuate_k(1, ps_a)
                    if has_tail(n, j, 2):
                        if due(tl - 1):
                            act.wait_ge(S["fm_ready"], tl - 1)
                        act.activation(fe[:], fe[:], ACT.Exp).then_inc(S["fe_ready"], 1)
                    if gat:
                        act.wait_ge(S["h_made"], tl + 1)
                        if due(tl):
                            act.wait_ge(S["thw_ready"], tl)
                        act.activation(th[:], ps_d[:, 1, 0:D], ACT.Tanh).then_inc(S["th_ready"], 1)
                    if tail:
                        exp1(tl - 1, 0)
                    if gat:
                        act.wait_ge(S["gate_made"], tl + 1)
                        if due(tl - 1):
                            act.wait_ge(S["r1_ready"], tl - 1)
                        act.activation(gate[:, j % 2, :], ps_d[:, 2, 0:D], ACT.Tanh,
                                       scale=0.5).then_inc(S["gate_ready"], 1)
                    if tail:
                        exp1(tl - 1, 1)
                    if qkv and n + 1 < NG and j == 3:
                        x_hi(g + 1, 0)
                    if att:
                        act.wait_ge(S["p0_turned"], ta + 1)
                        if due(ta):
                            act.wait_ge(S["ctx_made"], ta)
                        act.activation(p0T[:, 0, :, :], ps_s[:, 0, 0:C * N].rearrange("p (i n) -> p i n", i=C),
                                       ACT.Copy).then_inc(S["p0T_even"], 1)
                    if tail:
                        exp1(tl - 1, 2)
                    if qkv and j == 0:
                        evacuate_q(1, ps_b)
                    elif qkv and j == 1:
                        evacuate_k(0, ps_b)
                    elif qkv and j == 2:
                        evacuate_k(2, ps_b)
                    if att:
                        act.wait_ge(S["ctx_made"], ta + 1)
                        if due(ta):
                            act.wait_ge(S["out_made"], ta)
                        act.activation(ctxT[0][:], ps_a[:, 0:D].rearrange("p (c n) -> p c n", c=C),
                                       ACT.Copy).then_inc(S["ctx_hi"], 1)
                    if tail:
                        turned_p1(tl - 1, 0)
                    if gat:
                        act.wait_ge(S["d_turned"], tl + 1)
                        if due(tl):
                            act.wait_ge(S["logits_ready"], tl)
                        act.activation(dT[:], ps_c[0:3 * H1, 0:N // 2].bitcast(BF16), ACT.Copy).then_inc(S["dT_ready"], 1)
                    if tail:
                        turned_p1(tl - 1, 1)
                    if qkv and n + 1 < NG and j == 3:
                        x_hi(g + 1, 1)
            pipeline(act, iteration)

        @block_.vector
        def _(dve):
            dve.wait_ge(S["bias_in"], 32)
            dve.tensor_scalar(bq8[:], bq_col[:], D0 ** -0.5, None, ALU.mult).then_inc(S["bias_ready"], 1)
            for n, name in enumerate(W_ORDER):
                hi, lo = w_parts[name]
                dve.wait_ge(S["weight_hi"], n + 1)
                dve.tensor_tensor(lo[:], stage[n % 2], hi[:].bitcast(F32), ALU.subtract).then_inc(S["weight_lo"], 1)
                if n == 2:
                    dve.wait_ge(S["ident_in_ready"], 16)
                    dve.tensor_copy(ident_b[:], ident[:]).then_inc(S["consts_ready"], 1)
                    dve.tensor_scalar(ident_53[:], ident[:], 2.0 ** 53, None, ALU.mult).then_inc(S["consts_ready"], 1)
                    dve.tensor_scalar(ident_100[:], ident[:], 2.0 ** 100, None, ALU.mult).then_inc(S["consts_ready"], 1)
            dve.wait_ge(S["const_in"], 16 * 7)

            def iteration(g, par, n):
                qkv, att, gat = parts(n)

                def lo_part(parts_, source, at, name_hi, count, name_lo):
                    dve.wait_ge(S[name_hi], count)
                    dve.tensor_tensor(parts_[1][:, :, at], source[:, 0:D].rearrange("p (c n) -> p c n", c=C),
                                      parts_[0][:, :, at].bitcast(F32), ALU.subtract).then_inc(S[name_lo], 1)

                def evacuate_v(j, bank):
                    dve.wait_ge(S["v_made"], G * g + j + 1)
                    dve.tensor_tensor(v[:, par, j, :], bank[:, 0:D], bv_all[:], ALU.add).then_inc(S["v_ready"], 1)

                for j in range(G):
                    ta, tl = G * (g - 1) + j, G * (g - 2) + j
                    tt = tl - 1
                    tail = has_tail(n, j)
                    if att:
                        dve.wait_ge(S["scores_ready"], ta + 1)
                        dve.tensor_reduce(max0.rearrange("p (o i) -> p o i", o=2),
                                          ps_s[:, :, 0:C * N].rearrange("p o (i n) -> p o i n", i=C),
                                          AX_X, ALU.max).then_inc(S["att_small"], 1)
                        dve.wait_ge(S["att_small"], ta + 1)
                        if due(ta):
                            dve.wait_ge(S["exp0_ready"], ta)
                        dve.tensor_scalar(neg0, max0, -1.0, None, ALU.mult).then_inc(S["neg_ready"], 1)
                    if gat:
                        lo_part(x1T, ps_c, slice(0, N), "x1_hi", tl + 1, "x1_lo")
                    if qkv and j == 3:
                        for b in (0, 1):
                            evacuate_v(b, (ps_a, ps_b)[b])
                    if tail:
                        dve.wait_ge(S["z_ready"], tt + 1)
                        dve.scalar_tensor_tensor(z[:], z[:], 0.2, z[:], ALU.mult, ALU.max
                                                 ).then_inc(S["leaky_ready"], 1)
                        src_ = sd[:, (j + 1) % 2, 0, :]
                        dve.wait_ge(S["dmax_ready"], tt + 1)
                        dve.tensor_tensor(zmax, dmax, src_, ALU.add).then_inc(S["max1_small"], 1)
                        dve.wait_ge(S["max1_small"], 2 * tt + 1)
                        dve.scalar_tensor_tensor(m1, zmax, 0.2, zmax, ALU.mult, ALU.max).then_inc(S["max1_small"], 1)
                        dve.wait_ge(S["max1_small"], 2 * tt + 2)
                        if due(3 * tt):
                            dve.wait_ge(S["exp1_ready"], 3 * tt)
                        dve.tensor_scalar(neg1, m1, -1.0, None, ALU.mult).then_inc(S["neg1_ready"], 1)
                    if att:
                        dve.wait_ge(S["exp0_ready"], ta + 1)
                        if due(ta):
                            dve.wait_ge(S["p0_ready"], ta)
                        dve.reciprocal(inv0, sum0).then_inc(S["inv0_ready"], 1)
                    if has_tail(n, j, 2):
                        t2 = tl - 2
                        flat = lambda w: w[:].rearrange("p a e -> p (a e)")
                        x1_ = x1[:, par if j > 1 else 1 - par, (j - 2) % G, :]
                        dve.wait_ge(S["fe_ready"], t2 + 1)
                        if due(t2):
                            dve.wait_ge(S["y_ready"], t2)
                        dve.scalar_tensor_tensor(r1[:], flat(f), 0.0, flat(fe), ALU.max, ALU.add
                                                 ).then_inc(S["tail_small"], 1)
                        dve.wait_ge(S["tail_small"], 3 * t2 + 1)
                        dve.scalar_tensor_tensor(r1[:], r1[:], -1.0, x1_, ALU.add, ALU.subtract
                                                 ).then_inc(S["tail_small"], 1)
                        dve.wait_ge(S["tail_small"], 3 * t2 + 2)
                        dve.scalar_tensor_tensor(r1[:], gate[:, j % 2, :], 1.0, r1[:], ALU.add, ALU.mult
                                                 ).then_inc(S["tail_small"], 1)
                        dve.wait_ge(S["tail_small"], 3 * t2 + 3)
                        dve.scalar_tensor_tensor(r1[:], r1[:], 0.25, x1_, ALU.mult, ALU.add).then_inc(S["r1_ready"], 1)
                        dve.wait_ge(S["r1_ready"], t2 + 1)
                        dve.bn_stats(st1, r1[:]).then_inc(S["mv1_ready"], 1)
                        dve.wait_ge(S["mv1_ready"], apart(dve, 2 * t2 + 1))
                        dve.bn_aggr(mv1, st1).then_inc(S["mv1_ready"], 1)
                    if gat:
                        dve.wait_ge(S["th_ready"], tl + 1)
                        if due(tl - 1):
                            dve.wait_ge(S["ph_made"], tl - 1)
                        dve.tensor_copy(h[:, j % 2, :, 0:D1], ps_d[:, 1, 0:D].rearrange("p (a e) -> p a e", a=H1)
                                        ).then_inc(S["h_ready"], 1)
                    if att:
                        dve.wait_ge(S["p0_turned"], ta + 1)
                        if due(ta):
                            dve.wait_ge(S["ctx_made"], ta)
                        dve.tensor_copy(p0T[:, 1, :, :], ps_s[:, 1, 0:C * N].rearrange("p (i n) -> p i n", i=C)
                                        ).then_inc(S["p0T_odd"], 1)
                    if qkv and j == 3:
                        for b in (2, 3):
                            evacuate_v(b, (ps_a, ps_b)[b % 2])
                    if gat:
                        dve.wait_ge(S["thw_ready"], tl + 1)
                        dve.tensor_reduce(sd[:, j % 2, :, :], thw[:].rearrange("p s (a e) -> p s a e", a=H1), AX_X,
                                          ALU.add).then_inc(S["sd_ready"], 1)
                        dst = sd[:, j % 2, 1, :]
                        dve.wait_ge(S["sd_ready"], tl + 1)
                        if due(tl):
                            dve.wait_ge(S["d_turned"], tl)
                        dve.tensor_copy(dst3[:, 0, :], dst).then_inc(S["split_small"], 1)
                        dve.wait_ge(S["split_small"], 4 * tl + 1)
                        dve.tensor_tensor(dst_rest[:, 0, :], dst, dst3[:, 0, :], ALU.subtract).then_inc(S["split_small"], 1)
                        dve.wait_ge(S["split_small"], 4 * tl + 2)
                        dve.tensor_copy(dst3[:, 1, :], dst_rest[:, 0, :]).then_inc(S["split_small"], 1)
                        dve.wait_ge(S["split_small"], 4 * tl + 3)
                        dve.tensor_tensor(dst_rest[:, 1, :], dst_rest[:, 0, :], dst3[:, 1, :], ALU.subtract
                                          ).then_inc(S["split_small"], 1)
                        dve.wait_ge(S["split_small"], 4 * tl + 4)
                        dve.tensor_copy(dst3[:, 2, :], dst_rest[:, 1, :]).then_inc(S["dst3_ready"], 1)
                    if att:
                        dve.wait_ge(S["ctx_made"], ta + 1)
                        lo_part(ctxT, ps_a, slice(0, N), "ctx_hi", ta + 1, "ctx_lo")
                    if tail:
                        for q in (2,):
                            dve.wait_ge(S["p1_turned"], 3 * tt + q + 1)
                            if due(tt):
                                dve.wait_ge(S["ph_made"], tt)
                            dve.tensor_copy(p1T[:, 4 * q:4 * q + 4, :],
                                            ps_d[:, q, :].rearrange("p (a n) -> p a n", a=4)
                                            ).then_inc(S[f"p1T_{q}"], 1)
                    if att:
                        dve.wait_ge(S["out_made"], ta + 1)
                        dve.wait_ge(S["xb_ready"], 2 * (g - 1) + j // 2 + 1)
                        if due(ta):
                            dve.wait_ge(S["x1_ready"], ta)
                        dve.tensor_tensor(r0[:], ps_b[:, 0:D], xb[:, 1 - par, j, :], ALU.add).then_inc(S["r0_ready"], 1)
                        dve.wait_ge(S["r0_ready"], ta + 1)
                        dve.bn_stats(st0, r0[:]).then_inc(S["mv0_ready"], 1)
                        dve.wait_ge(S["mv0_ready"], apart(dve, 2 * ta + 1))
                        dve.bn_aggr(mv0, st0).then_inc(S["mv0_ready"], 1)
                    if gat:
                        src = sd[:, j % 2, 0, :]
                        dve.wait_ge(S["logits_ready"], tl + 1)
                        dve.tensor_reduce(dmax, ps_d[:, :, :].rearrange("p q (a n) -> p (q a) n", a=4), AX_X, ALU.max
                                          ).then_inc(S["dmax_ready"], 1)
                        if due(3 * tl):
                            dve.wait_ge(S["p1_turned"], 3 * tl)
                        dve.tensor_tensor(z[:], ps_d[:, :, :].rearrange("p q (a n) -> p (q a) n", a=4),
                                          src.unsqueeze(2).broadcast_to([P, H1, N]), ALU.add).then_inc(S["z_ready"], 1)
                    if tail:
                        ph = ps_c[:, 0:H1 * E1].rearrange("p (a e) -> p a e", a=H1)
                        dve.wait_ge(S["ph_made"], tt + 1)
                        dve.reciprocal(inv1.unsqueeze(2), ph[:, :, D1:E1]).then_inc(S["inv1_ready"], 1)
                        dve.wait_ge(S["inv1_ready"], tt + 1)
                        if due(3 * (tt - 1) + 1):
                            dve.wait_ge(S["tail_small"], 3 * (tt - 1) + 1)
                        dve.tensor_tensor(f[:], ph[:, :, 0:D1], inv1.unsqueeze(2).broadcast_to([P, H1, D1]),
                                          ALU.mult).then_inc(S["f0_ready"], 1)
            pipeline(dve, iteration)

        @block_.gpsimd
        def _(pool):
            def x_lo(g, half):
                at = slice(2 * half * N, 2 * (half + 1) * N)
                pool.wait_ge(S["x_hi"], 2 * g + half + 1)
                pool.tensor_tensor(xT[1][:, :, at], x_cols[:, :, at], xT[0][:, :, at].bitcast(F32), ALU.subtract
                                   ).then_inc(S["x_lo"], 1)

            pool.memset(minus_half[:], -0.5)
            pool.memset(ones_b[:], 1.0)
            for k in range(2):
                pool.memset(h[:, k, :, D1:E1], 1.0)
            x_lo(0, 0)
            x_lo(0, 1)
            for s in range(4):
                if due(s):
                    pool.wait_ge(S["mask_ready"], s)
                pool.dma_start(adj_u8, adj_dram[s]).then_inc(S["adj_in"], 16)
                pool.wait_ge(S["adj_in"], 16 * (s + 1))
                pool.tensor_scalar(mask[:, 16 * s:16 * s + 16, :], adj_u8, 1.0, -1.0, ALU.mult, ALU.add
                                   ).then_inc(S["mask_ready"], 1)
            pool.wait_ge(S["const_in"], 16 * 7)
            pool.tensor_copy(pick_b[:], pick).then_inc(S["pick_ready"], 1)
            pool.tensor_copy(hb_split[:, 0, :], hb_row).then_inc(S["hb_small"], 1)
            pool.wait_ge(S["hb_small"], 1)
            pool.tensor_tensor(hb_rest[:, 0, :], hb_row, hb_split[:, 0, :], ALU.subtract).then_inc(S["hb_small"], 1)
            pool.wait_ge(S["hb_small"], 2)
            pool.tensor_copy(hb_split[:, 1, :], hb_rest[:, 0, :]).then_inc(S["hb_small"], 1)
            pool.wait_ge(S["hb_small"], 3)
            pool.tensor_tensor(hb_rest[:, 1, :], hb_rest[:, 0, :], hb_split[:, 1, :], ALU.subtract
                               ).then_inc(S["hb_small"], 1)
            pool.wait_ge(S["hb_small"], 4)
            pool.tensor_copy(hb_split[:, 2, :], hb_rest[:, 1, :]).then_inc(S["hb_small"], 1)
            pool.wait_ge(S["hb_small"], 5)
            pool.dma_start(hb_rows[:], hb_split).then_inc(S["hb_moved"], 16)

            def normalise(r, mv, ve, rs, nm, eps, out_ap, small, count, done, ready):
                pool.tensor_scalar(ve, mv[:, 1:2], eps, None, ALU.add).then_inc(S[small], 1)
                pool.wait_ge(S[small], count + 1)
                pool.tensor_tensor(rs, ve, minus_half[:], ALU.pow).then_inc(S[small], 1)
                pool.wait_ge(S[small], apart(pool, count + 2))
                pool.tensor_scalar(nm, mv[:, 0:1], -1.0, None, ALU.mult).then_inc(S[small], 1)
                pool.wait_ge(S[small], apart(pool, count + 3))
                pool.tensor_scalar(out_ap, r, nm, rs, ALU.add, ALU.mult).then_inc(S[ready], 1)

            def iteration(g, par, n):
                qkv, att, gat = parts(n)
                for j in range(G):
                    ta, tl = G * (g - 1) + j, G * (g - 2) + j
                    tt = tl - 1
                    tail = has_tail(n, j)
                    if att:
                        pool.wait_ge(S["inv0_ready"], ta + 1)
                        pool.tensor_tensor(p0[:].rearrange("p o i n -> p (o i) n"),
                                           p0[:].rearrange("p o i n -> p (o i) n"),
                                           inv0.unsqueeze(2).broadcast_to([P, H0, N]), ALU.mult
                                           ).then_inc(S["p0_ready"], 1)
                    if gat:
                        pool.wait_ge(S["th_ready"], tl + 1)
                        if due(tl):
                            pool.wait_ge(S["sd_ready"], tl)
                        pool.tensor_tensor(thw[:], th[:].unsqueeze(1).broadcast_to([P, 2, D]), w_sd[:], ALU.mult
                                           ).then_inc(S["thw_ready"], 1)
                    if qkv and n + 1 < NG and j == 3:
                        x_lo(g + 1, 0)
                    if qkv and j in (1, 2):
                        at = slice(2 * j - 2, 2 * j)
                        pool.wait_ge(S["xb_in"], 16 * (g + 1))
                        pool.tensor_tensor(xb[:, par, at, :], xb[:, par, at, :],
                                           bf_all[:].unsqueeze(1).broadcast_to([P, 2, D]), ALU.add
                                           ).then_inc(S["xb_ready"], 1)
                    if has_tail(n, j, 2):
                        t2 = tl - 2
                        pool.wait_ge(S["mv1_ready"], apart(pool, 2 * t2 + 2))
                        if due(16 * (2 * (g - 2) + (j - 2) // 2)):
                            pool.wait_ge(S[f"y_stored_{j % 2}"], apart(pool, 16 * (2 * (g - 2) + (j - 2) // 2)))
                        normalise(r1[:], mv1, ve1, rs1, nm1, EPS / 4, y[:, j % 2, :], "ln1_small", 3 * t2, None,
                                  "y_ready")
                    if qkv and n + 1 < NG and j == 3:
                        x_lo(g + 1, 1)
                    if att:
                        pool.wait_ge(S["mv0_ready"], apart(pool, 2 * ta + 2))
                        if due(ta - 7):
                            pool.wait_ge(S["r1_ready"], apart(pool, ta - 7))
                        normalise(r0[:], mv0, ve0, rs0, nm0, EPS, x1[:, 1 - par, j, :], "ln0_small", 3 * ta, None,
                                  "x1_ready")
                    if tail:
                        pool.wait_ge(S["f0_ready"], tt + 1)
                        pool.tensor_tensor(f[:], f[:], b1_all[:].unsqueeze(1).broadcast_to([P, H1, D1]), ALU.add
                                           ).then_inc(S["f1_ready"], 1)
                        pool.wait_ge(S["f1_ready"], apart(pool, tt + 1))
                        if due(3 * (tt - 1) + 1):
                            pool.wait_ge(S["tail_small"], apart(pool, 3 * (tt - 1) + 1))
                        pool.tensor_scalar(fe[:], f[:], 0.0, None, ALU.min).then_inc(S["fm_ready"], 1)
            pipeline(pool, iteration)


def kernel(**inputs):
    import numpy as _np
    import concourse.bacc as _bacc
    from concourse import mybir as _mybir
    from concourse.bass_utils import run_bass_kernel_spmd as _run

    nc = _bacc.Bacc("TRN2", target_bir_lowering=False, num_devices=1)
    names = ["x", "adj"] + ["L0_gnn_" + n for n in ("Wq", "bq", "Wk", "bk", "Wv", "bv", "Wf", "bf")] + [
        "L1_gnn_" + n for n in ("W", "b", "w_src", "w_dst", "H_w", "H_b")]
    x_ = _np.asarray(inputs["x"])
    held = {"xT": x_.reshape(NG, G, N, C, P).transpose(0, 4, 3, 1, 2).reshape(NG, P, C, G * N)}
    held.update({n: _np.asarray(inputs[n]) for n in names})
    held["L1_gnn_H_w"] = held["L1_gnn_H_w"].T
    for n in ("L1_gnn_w_src", "L1_gnn_w_dst"):
        held[n] = held[n].reshape(D)
    for n in ("L0_gnn_bq", "L0_gnn_bk"):
        held[n] = held[n].reshape(C, P).T
    held["ident"] = _np.eye(P, dtype=_np.float32)
    row = _np.arange(3 * H1)[:, None, None] % H1
    held["pick"] = _np.broadcast_to(row == _np.arange(H1)[None, :, None], (3 * H1, H1, P)).astype(_np.float32)
    arrays, args = {}, []
    for name, a in held.items():
        a = _np.ascontiguousarray(a)
        arrays[f"in_{name}_dram"] = a
        args.append(nc.dram_tensor(f"in_{name}_dram", a.shape, _mybir.dt.from_np(a.dtype), kind="ExternalInput").ap())
    out = nc.dram_tensor("out_0_dram", (B, N, D), F32, kind="ExternalOutput").ap()
    build_program(nc, *args, out)
    r = _run(nc, [arrays], core_ids=[0])
    return r.results[0]["out_0_dram"]
```

```python
from contextlib import ExitStack

import concourse.bass as bass
from concourse import mybir

ALU = mybir.AluOpType
ACT = mybir.ActivationFunctionType
F32 = mybir.dt.float32
F32R = mybir.dt.float32r
BF16 = mybir.dt.bfloat16
AX_X = mybir.AxisListType.X

B, N, D = 64, 128, 384
P = 128
C = D // P
G = 4
NG = B // G
H0, D0 = 6, 64
H1, D1 = 12, 32
EPS = 1e-5
HI_LO = ((0, 0), (1, 0), (0, 1))


def build_program(nc, xT_in, x, adj, Wq, bq, Wk, bk, Wv, bv, Wf, bf, W1, b1, w_src, w_dst, HwT, Hb,
                  ident_in, pick_in, out):
    with ExitStack() as ctx:
        def sb(name, shape, dt=F32):
            return ctx.enter_context(nc.sbuf_tensor(name, shape, dt))

        def psum(name, shape, dt=F32):
            return ctx.enter_context(nc.psum_tensor(name, shape, dt))

        def sem(name):
            return ctx.enter_context(nc.semaphore(name))

        ps_a = psum("ps_a", [P, 512])
        ps_b = psum("ps_b", [P, 512])
        ps_s = psum("ps_s", [P, 2, 512])
        ps_c = psum("ps_c", [P, 512])
        ps_d = psum("ps_d", [P, 3, 512])

        ident = sb("ident", [P, P])
        ident_b = sb("ident_b", [P, P], BF16)
        ident_53 = sb("ident_53", [P, P], BF16)
        ident_100 = sb("ident_100", [P, P], BF16)
        pick_b = sb("pick_b", [3 * H1, H1, P], BF16)
        ones_b = sb("ones_b", [3, P], BF16)
        minus_half = sb("minus_half", [P, 1])
        minus_one = sb("minus_one", [P, 1])
        w_parts = {n: [sb(f"{n}_hi", [P, C, D], F32R), sb(f"{n}_lo", [P, C, D], F32R)]
                   for n in ("wq", "wk", "wv", "wf", "w1", "hw")}
        bq_col = sb("bq_col", [P, C])
        bq8 = sb("bq8", [P, C])
        bk_col = sb("bk_col", [P, C])
        bv_col = sb("bv_col", [P, C])
        bf_all = sb("bf_all", [P, D])
        b1_all = sb("b1_all", [P, D1])
        w_sd = sb("w_sd", [P, 2, D])
        hb_rows = sb("hb_rows", [3, D], BF16)
        mask = sb("mask", [P, B, N], BF16)

        x_cols = sb("x_cols", [P, C, G * N])
        xT = [sb("xT_hi", [P, C, G * N], F32R), sb("xT_lo", [P, C, G * N], F32R)]
        xb = sb("xb", [P, 2, G, D])
        qT = sb("qT", [P, 2, C, G * N])
        kT = sb("kT", [P, 2, C, G * N])
        v = sb("v", [P, 2, G, D])
        p0 = sb("p0", [P, 2, C, N])
        p0T = sb("p0T", [P, 2, C, N])
        ctxT = [sb("ctxT_hi", [P, C, N], F32R), sb("ctxT_lo", [P, C, N], F32R)]
        r0 = sb("r0", [P, D])
        s0 = sb("s0", [P, 64])
        max0, neg0, sum0, inv0 = (s0[:, 8 * k:8 * k + H0] for k in range(4))
        st0, mv0, ve0, rs0, nm0 = s0[:, 32:38], s0[:, 40:42], s0[:, 44:45], s0[:, 46:47], s0[:, 48:49]
        x1 = sb("x1", [P, 2, G, D])
        x1T = [sb("x1T_hi", [P, C, N], F32R), sb("x1T_lo", [P, C, N], F32R)]
        h = sb("h", [P, 2, H1, D1])
        th = sb("th", [P, D])
        gate = sb("gate", [P, 2, D])
        thw = sb("thw", [P, 2, D])
        sd = sb("sd", [P, 2, H1])
        sd_rest = sb("sd_rest", [P, 2, 2, H1])
        sd3 = sb("sd3", [P, 2, 3, H1], BF16)
        sdT = sb("sdT", [3 * H1, 2, N], BF16)
        z = sb("z", [P, H1, N])
        s1 = sb("s1", [P, 64])
        zmax, neg1 = s1[:, 0:H1], s1[:, 16:16 + H1]
        p1T = sb("p1T", [P, H1, N])
        s2 = sb("s2", [P, 64])
        inv1, sum1 = s2[:, 0:12], s2[:, 40:52]
        st1, mv1, ve1, rs1, nm1 = s2[:, 16:22], s2[:, 24:26], s2[:, 28:29], s2[:, 30:31], s2[:, 32:33]
        fT = sb("fT", [P, C, N])
        f = sb("f", [P, H1, D1])
        fe = sb("fe", [P, D])
        r1 = sb("r1", [P, D])
        y = sb("y", [P, 2, D])
        def staging(buffer):
            return buffer.rearrange("p a n -> p (a n)")[:, 0:C * D].rearrange("p (c n) -> p c n", c=C)

        stage = [staging(z[:, :, :]), staging(p1T[:, :, :]), staging(qT[:, 1, :, :]), staging(kT[:, 1, :, :])]
        pick = v[:, 1, :, :].rearrange("p j d -> p (j d)")[0:3 * H1, :].rearrange("p (a n) -> p a n", a=H1)
        bf_in = th[:]
        hb_row = r1[0:1, :]
        hb_rest = y[0:1, :, :]
        hb_split = gate[0:1, :, :].rearrange("p a d -> p (a d)").bitcast(BF16)[:, 0:3 * D].rearrange("p (a d) -> p a d", a=3)
        adj_u8 = x1[:].rearrange("p a j d -> p (a j d)")[:, 0:B * N // 4].bitcast(mybir.dt.uint8
                                                                          ).rearrange("p (b n) -> p b n", n=N)

        names = """ident_in_ready const_in weight_in_0 weight_in_1 weight_in_2 weight_in_3 weight_in_4 weight_in_5 late_hi bvf_made bf_ready adj_in x_in_ready weight_hi weight_lo mask_ready consts_ready pick_ready hb_moved
            bias_in bias_ready hb_small x_hi x_lo x_lo_first xb_in xb_ready q_made k_made qk_a_ready qk_b_ready v_made v_even v_odd
            scores_ready att_small neg_ready exp0_ready inv0_ready p0_ready p0_turned p0T_even p0T_odd
            ctx_made ctx_hi ctx_lo out_made r0_ready mv0_ready ln0_small x1_ready
            x1_turned x1_hi x1_lo h_made h_ready th_ready gate_made gate_ready thw_ready
            sd_ready split_small sd3_ready sd_turned sdT_ready logits_ready relu_ready z_ready zmax_ready neg1_ready
            exp1_ready p1_turned p1T_0 p1T_1 p1T_2 ph_made fT_ready f_turned inv1_ready f0_ready f1_ready minus_one_ready b1_ready
            fe_ready tail_small r1_ready mv1_ready ln1_small y_ready y_stored_0 y_stored_1"""
        S = {n: sem(n) for n in names.split()}

        def due(value):
            return not isinstance(value, int) or value > 0

        def apart(eng, value):
            if not isinstance(value, int):
                value = eng.to_reg(value)
                eng.wait_ge(S["ident_in_ready"], 16)
            return value

        W_ORDER = ["wq", "wk", "wv", "wf", "w1", "hw"]
        DRAM_W = {"wq": Wq, "wk": Wk, "wv": Wv, "wf": Wf, "w1": W1, "hw": HwT}
        x_dram = x.rearrange("(g b) n d -> g n b d", b=G)
        adj_dram = adj.rearrange("b n m -> n b m")
        out_dram = out

        def pipeline(eng, iteration):
            for g in (0, 1, 2):
                iteration(g, g % 2, g)
            with eng.Fori(0, (NG - 4) // 2) as pair:
                iteration(pair * 2 + 3, 1, 3)
                iteration(pair * 2 + 4, 0, 4)
            for g in range(NG - 1, NG + 3):
                iteration(g, g % 2, g)

        def parts(n):
            return n < NG, 1 <= n <= NG, 2 <= n <= NG + 1

        def has_tail(n, j, lag=1):
            return 0 <= G * (n - 2) + j - lag < B

        block_ = ctx.enter_context(nc.Block())

        @block_.sync
        def _(sp):
            sp.dma_start(x_cols[:], xT_in[0]).then_inc(S["x_in_ready"], 16)
            for n, name in enumerate(W_ORDER):
                if n >= 4:
                    sp.wait_ge(S["weight_lo"], n - 3)
                sp.dma_start(stage[n % 4], DRAM_W[name].rearrange("(c p) n -> p c n", p=P)
                             ).then_inc(S[f"weight_in_{n}"], 16)

            def iteration(g, par, n):
                qkv, att, gat = parts(n)
                xb_and_x_lo, residuals = 2 * g, G * (g - 1)
                if not isinstance(g, int):
                    xb_and_x_lo, residuals = sp.to_reg(xb_and_x_lo), sp.to_reg(residuals)
                if qkv:
                    if due(G * (g - 1)):
                        sp.wait_ge(S["r0_ready"], residuals)
                    if due(2 * g):
                        sp.wait_ge(S["xb_ready"], xb_and_x_lo)
                    sp.dma_start(xb[:, par, :, :], x_dram[g] if isinstance(g, int)
                                 else x_dram[bass.ds(g, 1)].rearrange("o n b d -> (o n) b d")
                                 ).then_inc(S["xb_in"], 16)
                if n + 1 < NG:
                    following = xT_in[g + 1] if isinstance(g, int) else \
                        xT_in[bass.ds(g + 1, 1)].rearrange("o p c n -> (o p) c n")
                    if n == 0:
                        sp.wait_ge(S["x_lo_first"], 2)
                    else:
                        sp.wait_ge(S["x_lo"], xb_and_x_lo)
                    sp.dma_start(x_cols[:], following).then_inc(S["x_in_ready"], 16)
                for j in range(G):
                    if has_tail(n, j, 2):
                        t = G * (g - 2) + j - 2
                        sp.wait_ge(S["y_ready"], t + 1)
                        dst = out_dram[t] if isinstance(t, int) else out_dram[bass.ds(t, 1)].rearrange("o n d -> (o n) d")
                        sp.dma_start(dst, y[:, j % 2, :]).then_inc(S[f"y_stored_{j % 2}"], 16)
            pipeline(sp, iteration)
            for k in range(2):
                sp.wait_ge(S[f"y_stored_{k}"], 16 * B // 2)

        @block_.tensor
        def _(pe):
            def split_product(out_ap, lhs, rhs, chunks=range(C), closed=True):
                for c in chunks:
                    for k, (a, b) in enumerate(HI_LO):
                        last = pe.matmul(out_ap, lhs(a, c), rhs(b, c), start=(c == 0 and k == 0),
                                         stop=(closed and c == C - 1 and k == 2))
                return last

            def project_qk(name, m, bank):
                split_product(bank[:], lambda a, c: w_parts[name][a][:, c, m * P:(m + 1) * P],
                              lambda b, c: xT[b][:, c, :]).then_inc(S["q_made" if name == "wq" else "k_made"], 1)

            def project_v(j, bank):
                split_product(bank[:, 0:D], lambda a, c: xT[a][:, c, j * N:(j + 1) * N],
                              lambda b, c: w_parts["wv"][b][:, c, :]).then_inc(S["v_made"], 1)

            def fill_a(g, n, j):
                if j == 0:
                    if n == 0:
                        pe.wait_ge(S["x_lo_first"], 2)
                    else:
                        pe.wait_ge(S["x_lo"], 2 * g)
                    if due(g):
                        pe.wait_ge(S["v_even"], 2 * g)
                        pe.wait_ge(S["v_odd"], 2 * g)
                if parts(n)[1]:
                    if due(G * (g - 1) + j):
                        pe.wait_ge(S["ctx_lo"], G * (g - 1) + j)
                if j == 0:
                    if n == 0:
                        pe.wait_ge(S["weight_lo"], 1)
                    project_qk("wq", 0, ps_a)
                elif j == 1:
                    pe.wait_ge(S["qk_a_ready"], 3 * g + 1)
                    project_qk("wq", 2, ps_a)
                elif j == 2:
                    pe.wait_ge(S["qk_a_ready"], 3 * g + 2)
                    project_qk("wk", 1, ps_a)
                else:
                    if n == 0:
                        pe.wait_ge(S["weight_lo"], 3)
                    pe.wait_ge(S["qk_a_ready"], 3 * g + 3)
                    project_v(0, ps_a)
                    if parts(n)[1]:
                        if due(G * (g - 1) + j):
                            pe.wait_ge(S["r0_ready"], G * (g - 1) + j)
                    if parts(n)[2]:
                        pe.wait_ge(S["x1_lo"], G * (g - 2) + j + 1)
                    pe.wait_ge(S["qk_b_ready"], 3 * g + 3)
                    project_v(1, ps_b)

            def fill_b(g, n, j):
                if j == 3:
                    pe.wait_ge(S["v_even"], 2 * g + 1)
                    project_v(2, ps_a)
                    pe.wait_ge(S["v_odd"], 2 * g + 1)
                    project_v(3, ps_b)
                    return
                if parts(n)[1]:
                    if due(G * (g - 1) + j):
                        pe.wait_ge(S["r0_ready"], G * (g - 1) + j)
                if j == 1:
                    pe.wait_ge(S["qk_b_ready"], 3 * g + 1)
                    if n == 0:
                        pe.wait_ge(S["weight_lo"], 2)
                elif j == 2:
                    pe.wait_ge(S["qk_b_ready"], 3 * g + 2)
                project_qk(*(("wq", 1), ("wk", 0), ("wk", 2))[j], ps_b)

            def bias_product():
                pe.wait_ge(S["weight_lo"], 4)
                pe.wait_ge(S["const_in"], 16 * 7)
                for c in range(C):
                    for k in range(2):
                        last = pe.matmul(ps_s[:, 0, 0:D], bv_col[:, c:c + 1].broadcast_to([P, P]),
                                         w_parts["wf"][k][:, c, :].bitcast(F32), start=(c == 0 and k == 0),
                                         stop=(c == C - 1 and k == 1))
                last.then_inc(S["bvf_made"], 1)

            def scores(t, g, par, j):
                if due(t):
                    pe.wait_ge(S["p0T_even"], t)
                if due(t):
                    pe.wait_ge(S["p0T_odd"], t)
                if j == 0:
                    pe.wait_ge(S["qk_a_ready"], 3 * g)
                    pe.wait_ge(S["qk_b_ready"], 3 * g)
                m = mask[:, t, :].unsqueeze(1) if isinstance(t, int) else mask[:, bass.ds(t, 1), :]
                for o in range(2):
                    pe.matmul(ps_s[:, o, 0:C * N].rearrange("p (i n) -> p i n", i=C), ident_53[:],
                              m.broadcast_to([P, C, N]), start=True, stop=False)
                for i in range(C):
                    for o in range(2):
                        q_, k_ = (w[D0 * o:D0 * (o + 1), par, i, j * N:(j + 1) * N] for w in (qT, kT))
                        last = pe.matmul(ps_s[:, o, i * N:(i + 1) * N], q_, k_, start=False, stop=(i == C - 1))
                last.then_inc(S["scores_ready"], 1)

            def turn_p0(t):
                pe.wait_ge(S["p0_ready"], t + 1)
                for o in range(2):
                    for i in range(C):
                        last = pe.transpose(ps_s[:, o, i * N:(i + 1) * N], p0[:, o, i, :], ident[:])
                last.then_inc(S["p0_turned"], 1)

            def context(t, g, par, j, n):
                if j == 0:
                    pe.wait_ge(S["v_even"], 2 * g)
                    pe.wait_ge(S["v_odd"], 2 * g)
                if parts(n)[0]:
                    if j < 3:
                        pe.wait_ge(S["qk_a_ready"], 3 * g + j + 1)
                    else:
                        pe.wait_ge(S["v_even"], 2 * g + 2)
                else:
                    if due(t):
                        pe.wait_ge(S["ctx_lo"], t)
                pe.wait_ge(S["p0T_even"], t + 1)
                pe.wait_ge(S["p0T_odd"], t + 1)
                for i in range(C):
                    for o in range(2):
                        hd = 2 * i + o
                        last = pe.matmul(ps_a[D0 * o:D0 * (o + 1), i * N:(i + 1) * N],
                                         v[:, par, j, hd * D0:(hd + 1) * D0], p0T[:, o, i, :], start=True, stop=True)
                last.then_inc(S["ctx_made"], 1)

            def project_out(t, g, j, n, chunks):
                if chunks[0] == 0:
                    if parts(n)[0]:
                        if j < 3:
                            pe.wait_ge(S["qk_b_ready"], 3 * g + j + 1)
                        else:
                            pe.wait_ge(S["v_odd"], 2 * g + 2)
                    elif due(t):
                        pe.wait_ge(S["r0_ready"], t)
                    pe.wait_ge(S["ctx_lo"], t + 1)
                    if n == 1 and j == 0:
                        pe.wait_ge(S["weight_lo"], 4)
                last = split_product(ps_b[:, 0:D], lambda a, c: ctxT[a][:, c, :],
                                     lambda b, c: w_parts["wf"][b][:, c, :], chunks)
                if chunks[-1] == C - 1:
                    last.then_inc(S["out_made"], 1)

            def turn_x1(t, par, j, has_att):
                if due(t + G):
                    pe.wait_ge(S["r0_ready"], t + G if has_att else B)
                pe.wait_ge(S["x1_ready"], t + 1)
                for c in range(C):
                    last = pe.transpose(ps_b[:, c * P:(c + 1) * P], x1[:, par, j, c * P:(c + 1) * P], ident[:])
                last.then_inc(S["x1_turned"], 1)

            def project_h(t, n, j):
                pe.wait_ge(S["x1_lo"], t + 1)
                if due(t):
                    pe.wait_ge(S["z_ready"], 3 * t)
                if n == 2 and j == 0:
                    pe.wait_ge(S["weight_lo"], 6)
                    pe.wait_ge(S["hb_moved"], 16)
                    pe.wait_ge(S["pick_ready"], 1)
                split_product(ps_d[:, 1, 0:D], lambda a, c: x1T[a][:, c, :],
                              lambda b, c: w_parts["w1"][b][:, c, :]).then_inc(S["h_made"], 1)

            def project_gate(chunks):
                split_product(ps_d[:, 2, 0:D], lambda a, c: x1T[a][:, c, :],
                              lambda b, c: w_parts["hw"][b][:, c, :], chunks, closed=False)
                if chunks[-1] == C - 1:
                    pe.matmul(ps_d[:, 2, 0:D], ones_b[:], hb_rows[:], start=False, stop=True
                              ).then_inc(S["gate_made"], 1)

            def turn_sd(t):
                if due(t - 1):
                    pe.wait_ge(S["f0_ready"], apart(pe, t - 1))
                pe.wait_ge(S["sd3_ready"], apart(pe, t + 1))
                for k in range(2):
                    last = pe.transpose(ps_c[0:3 * H1, k * N // 2:(k + 1) * N // 2].bitcast(BF16),
                                        sd3[:, k, :, :].rearrange("p s a -> p (s a)"), ident_b[:])
                last.then_inc(S["sd_turned"], 1)

            def logits(t):
                pe.wait_ge(S["h_ready"], t + 1)
                pe.wait_ge(S["gate_ready"], t + 1)
                pe.wait_ge(S["sdT_ready"], t + 1)
                m = mask[:, t, :].unsqueeze(1) if isinstance(t, int) else mask[:, bass.ds(t, 1), :]
                for q in range(3):
                    if due(t):
                        pe.wait_ge(S[f"p1T_{q}"], t)
                    heads = ps_d[:, q, :].rearrange("p (a n) -> p a n", a=4)
                    pe.matmul(heads, ident_100[:], m.broadcast_to([P, 4, N]), start=True, stop=False)
                    pe.matmul(heads, sdT[:, 0, :], pick_b[:, 4 * q:4 * q + 4, :], start=False, stop=False)
                    for a in range(4 * q, 4 * q + 4):
                        last = pe.matmul(ps_d[:, q, (a % 4) * N:(a % 4 + 1) * N], pick_b[:, a, :], sdT[:, 1, :],
                                         start=False, stop=(a % 4 == 3))
                    last.then_inc(S["logits_ready"], 1)

            def turn_p1(t, next_is_here, groups):
                for q in groups:
                    if next_is_here and q == 1:
                        pe.wait_ge(S["h_ready"], t + 2)
                    if next_is_here and q == 2:
                        pe.wait_ge(S["gate_ready"], t + 2)
                    pe.wait_ge(S["exp1_ready"], 3 * t + q + 1)
                    for a in range(4 * q, 4 * q + 4):
                        last = pe.transpose(ps_d[:, q, (a % 4) * N:(a % 4 + 1) * N], z[:, a, :], ident[:])
                    last.then_inc(S["p1_turned"], 1)

            def apply_p1(t, par2, next_is_here):
                if next_is_here:
                    pe.wait_ge(S["sdT_ready"], t + 2)
                elif due(t):
                    pe.wait_ge(S["f0_ready"], t)
                for q in range(3):
                    pe.wait_ge(S[f"p1T_{q}"], t + 1)
                    for a in range(4 * q, 4 * q + 4):
                        last = pe.matmul(ps_c[D1 * (a % 4):D1 * (a % 4 + 1), q * N:(q + 1) * N],
                                         h[:, par2, a, :], p1T[:, a, :], start=True, stop=True)
                last.then_inc(S["ph_made"], 1)

            def turn_f(t):
                pe.wait_ge(S["fT_ready"], t + 1)
                for c in range(C):
                    last = pe.transpose(ps_c[:, c * P:(c + 1) * P], fT[:, c, :], ident[:])
                last.then_inc(S["f_turned"], 1)

            def iteration(g, par, n):
                qkv, att, gat = parts(n)
                for j in range(G):
                    ta, tl = G * (g - 1) + j, G * (g - 2) + j
                    tail = has_tail(n, j)
                    if att:
                        if n == 1 and j == 0:
                            pe.wait_ge(S["consts_ready"], 3)
                            pe.wait_ge(S["mask_ready"], 4)
                            pe.wait_ge(S["bf_ready"], 1)
                        scores(ta, g, 1 - par, j)
                    if has_tail(n, j, 2):
                        turn_f(tl - 2)
                    if gat:
                        turn_x1(tl, par, j, att)
                    if n == 0 and j == 3:
                        bias_product()
                    if qkv:
                        fill_a(g, n, j)
                    if gat:
                        project_h(tl, n, j)
                    if qkv:
                        fill_b(g, n, j)
                    if att:
                        turn_p0(ta)
                    if gat:
                        project_gate((0,))
                    if tail:
                        turn_p1(tl - 1, gat, (0,))
                    if att:
                        context(ta, g, 1 - par, j, n)
                    if gat:
                        project_gate((1,))
                    if tail:
                        turn_p1(tl - 1, gat, (1,))
                    if gat:
                        project_gate((2,))
                    if att:
                        project_out(ta, g, j, n, (0, 1))
                    if gat:
                        turn_sd(tl)
                    if tail:
                        turn_p1(tl - 1, gat, (2,))
                    if att:
                        project_out(ta, g, j, n, (2,))
                    if gat:
                        logits(tl)
                    if tail:
                        apply_p1(tl - 1, (j + 1) % 2, gat)
            pipeline(pe, iteration)

        @block_.scalar
        def _(act):
            act.dma_start(bq_col[:], bq).then_inc(S["bias_in"], 16)
            act.dma_start(bk_col[:], bk).then_inc(S["bias_in"], 16)
            act.dma_start(ident[:], ident_in).then_inc(S["ident_in_ready"], 16)
            act.dma_start(adj_u8, adj_dram).then_inc(S["adj_in"], 16)
            act.dma_start(bv_col[:], bv).then_inc(S["const_in"], 16)
            act.dma_start(pick, pick_in).then_inc(S["const_in"], 16)
            for s, w in enumerate((w_src, w_dst)):
                act.dma_start(w_sd[:, s, :], w.partition_broadcast(P)).then_inc(S["const_in"], 16)
            act.dma_start(bf_in, bf.partition_broadcast(P)).then_inc(S["const_in"], 16)
            act.dma_start(b1_all[:], b1.partition_broadcast(P)).then_inc(S["const_in"], 16)
            act.dma_start(hb_row, Hb.rearrange("(o d) -> o d", o=1)).then_inc(S["const_in"], 16)
            act.wait_ge(S["minus_one_ready"], 1)
            act.activation(s2[:, 60:61], minus_one[:], ACT.Exp)
            act.wait_ge(S["bias_in"], 32)
            act.activation(bq8[:], bq_col[:], ACT.Copy, scale=D0 ** -0.5).then_inc(S["bias_ready"], 1)

            def x_hi(g, half):
                at = slice(2 * half * N, 2 * (half + 1) * N)
                act.wait_ge(S["x_in_ready"], 16 * (g + 1))
                if due(G * (g - 1) + 2 * (half + 1)):
                    act.wait_ge(S["v_made"], G * (g - 1) + 2 * (half + 1))
                act.activation(xT[0][:, :, at], x_cols[:, :, at], ACT.Copy).then_inc(S["x_hi"], 1)

            x_hi(0, 0)
            x_hi(0, 1)
            for n in range(3):
                act.wait_ge(S[f"weight_in_{n}"], 16)
                act.activation(w_parts[W_ORDER[n]][0][:], stage[n], ACT.Copy).then_inc(S["weight_hi"], 1)
            act.wait_ge(S["bias_ready"], 1)

            def iteration(g, par, n):
                qkv, att, gat = parts(n)

                def evacuate_q(m, bank):
                    act.wait_ge(S["q_made"], 3 * g + m + 1)
                    act.activation(qT[:, par, m, :], bank[:], ACT.Identity, bias=bq8[:, m:m + 1],
                                   scale=D0 ** -0.5).then_inc(S["qk_a_ready"], 1)

                def evacuate_k(m, bank):
                    act.wait_ge(S["k_made"], 3 * g + m + 1)
                    act.activation(kT[:, par, m, :], bank[:], ACT.Identity,
                                   bias=bk_col[:, m:m + 1]).then_inc(S["qk_a_ready"], 1)

                def evacuate_v(j):
                    act.wait_ge(S["v_made"], G * g + j + 1)
                    act.activation(v[:, par, j, :], ps_a[:, 0:D], ACT.Copy).then_inc(S["v_even"], 1)

                def exp1(t, first, end):
                    if first == 0:
                        act.wait_ge(S["neg1_ready"], t + 1)
                    for a in range(first, end):
                        done = act.activation(z[:, a, :], z[:, a, :], ACT.Exp, bias=neg1[:, a:a + 1],
                                              accum_out=sum1[:, a:a + 1])
                        if a % 4 == 3:
                            done.then_inc(S["exp1_ready"], 1)

                def turned_p1(t, q):
                    act.wait_ge(S["p1_turned"], 3 * t + q + 1)
                    if due(t):
                        act.wait_ge(S["ph_made"], t)
                    act.activation(p1T[:, 4 * q:4 * q + 4, :], ps_d[:, q, :].rearrange("p (a n) -> p a n", a=4),
                                   ACT.Copy).then_inc(S[f"p1T_{q}"], 1)

                for j in range(G):
                    ta, tl = G * (g - 1) + j, G * (g - 2) + j
                    tail = has_tail(n, j)
                    if gat:
                        act.wait_ge(S["x1_turned"], tl + 1)
                        act.activation(x1T[0][:], ps_b[:, 0:D].rearrange("p (c n) -> p c n", c=C),
                                       ACT.Copy).then_inc(S["x1_hi"], 1)
                    if att:
                        act.wait_ge(S["neg_ready"], ta + 1)
                        if due(ta):
                            act.wait_ge(S["p0_turned"], ta)
                        for o in range(2):
                            for i in range(C):
                                k = C * o + i
                                last = act.activation(p0[:, o, i, :], ps_s[:, o, i * N:(i + 1) * N], ACT.Exp,
                                                      bias=neg0[:, k:k + 1], accum_out=sum0[:, k:k + 1])
                        last.then_inc(S["exp0_ready"], 1)
                    if qkv and j == 0:
                        evacuate_q(0, ps_a)
                    elif qkv and j == 1:
                        evacuate_q(2, ps_a)
                    elif qkv and j == 2:
                        evacuate_k(1, ps_a)
                    elif qkv:
                        evacuate_v(0)
                    if has_tail(n, j, 2):
                        act.wait_ge(S["f1_ready"], tl - 1)
                        if due(tl - 2):
                            act.wait_ge(S["tail_small"], 3 * (tl - 3) + 1)
                        act.activation(fe[:], f[:].rearrange("p a e -> p (a e)"), ACT.Exp, bias=minus_one[:]
                                       ).then_inc(S["fe_ready"], 1)
                    if gat:
                        act.wait_ge(S["h_made"], tl + 1)
                        if due(tl):
                            act.wait_ge(S["thw_ready"], tl)
                        act.activation(th[:], ps_d[:, 1, 0:D], ACT.Tanh).then_inc(S["th_ready"], 1)
                    if tail:
                        exp1(tl - 1, 0, 4)
                    if qkv and j == 3:
                        evacuate_v(2)
                    if att:
                        act.wait_ge(S["p0_turned"], ta + 1)
                        if due(ta):
                            act.wait_ge(S["ctx_made"], ta)
                        act.activation(p0T[:, 0, :, :], ps_s[:, 0, 0:C * N].rearrange("p (i n) -> p i n", i=C),
                                       ACT.Copy).then_inc(S["p0T_even"], 1)
                    if tail:
                        exp1(tl - 1, 4, 8)
                    if att:
                        act.wait_ge(S["ctx_made"], ta + 1)
                        if due(ta):
                            act.wait_ge(S["out_made"], ta)
                        act.activation(ctxT[0][:], ps_a[:, 0:D].rearrange("p (c n) -> p c n", c=C),
                                       ACT.Copy).then_inc(S["ctx_hi"], 1)
                    if tail:
                        exp1(tl - 1, 8, 12)
                    if gat:
                        act.wait_ge(S["gate_made"], tl + 1)
                        if due(tl - 1):
                            act.wait_ge(S["tail_small"], 3 * (tl - 1))
                        act.activation(gate[:, j % 2, :], ps_d[:, 2, 0:D], ACT.Tanh,
                                       scale=0.5).then_inc(S["gate_ready"], 1)
                    if gat:
                        act.wait_ge(S["sd_turned"], tl + 1)
                        if due(tl):
                            act.wait_ge(S["logits_ready"], 3 * tl)
                        act.activation(sdT[:], ps_c[0:3 * H1, 0:N].bitcast(BF16).rearrange("p (s n) -> p s n", s=2),
                                       ACT.Copy).then_inc(S["sdT_ready"], 1)
                    if tail:
                        turned_p1(tl - 1, 1)
                    if qkv and n + 1 < NG and j == 3:
                        x_hi(g + 1, 0)
                        x_hi(g + 1, 1)
                    if gat:
                        for q in range(3):
                            act.wait_ge(S["logits_ready"], 3 * tl + q + 1)
                            if due(tl):
                                act.wait_ge(S["p1_turned"], 3 * (tl - 1) + q + 1)
                            act.activation(z[:, 4 * q:4 * q + 4, :], ps_d[:, q, :].rearrange("p (a n) -> p a n", a=4),
                                           ACT.Relu, scale=0.8).then_inc(S["relu_ready"], 1)
                    if tail:
                        act.wait_ge(S["ph_made"], tl)
                        if due(tl - 1):
                            act.wait_ge(S["f_turned"], tl - 1)
                        act.activation(fT[:], ps_c[:, 0:D].rearrange("p (c n) -> p c n", c=C),
                                       ACT.Copy).then_inc(S["fT_ready"], 1)
            pipeline(act, iteration)

        @block_.vector
        def _(dve):
            dve.wait_ge(S["bias_ready"], 1)
            for half in range(2):
                at = slice(2 * half * N, 2 * (half + 1) * N)
                dve.wait_ge(S["x_hi"], half + 1)
                dve.tensor_tensor(xT[1][:, :, at], x_cols[:, :, at], xT[0][:, :, at].bitcast(F32), ALU.subtract
                                  ).then_inc(S["x_lo_first"], 1)

            def weight_parts(n):
                hi, lo = w_parts[W_ORDER[n]]
                if n < 3:
                    dve.wait_ge(S["weight_hi"], n + 1)
                else:
                    dve.wait_ge(S[f"weight_in_{n}"], 16)
                    dve.tensor_copy(hi[:], stage[n % 4]).then_inc(S["late_hi"], 1)
                    dve.wait_ge(S["late_hi"], n - 2)
                dve.tensor_tensor(lo[:], stage[n % 4], hi[:].bitcast(F32), ALU.subtract).then_inc(S["weight_lo"], 1)

            def small_constants():
                dve.wait_ge(S["ident_in_ready"], 16)
                dve.tensor_copy(ident_b[:], ident[:]).then_inc(S["consts_ready"], 1)
                dve.tensor_scalar(ident_53[:], ident[:], 2.0 ** 53, None, ALU.mult).then_inc(S["consts_ready"], 1)
                dve.tensor_scalar(ident_100[:], ident[:], 2.0 ** 100, None, ALU.mult).then_inc(S["consts_ready"], 1)
                dve.wait_ge(S["const_in"], 16 * 7)
                dve.tensor_copy(pick_b[:], pick).then_inc(S["pick_ready"], 1)
                dve.tensor_copy(hb_split[:, 0, :], hb_row).then_inc(S["hb_small"], 1)
                dve.wait_ge(S["hb_small"], 1)
                dve.tensor_tensor(hb_rest[:, 0, :], hb_row, hb_split[:, 0, :], ALU.subtract).then_inc(S["hb_small"], 1)
                dve.wait_ge(S["hb_small"], 2)
                dve.tensor_copy(hb_split[:, 1, :], hb_rest[:, 0, :]).then_inc(S["hb_small"], 1)
                dve.wait_ge(S["hb_small"], 3)
                dve.tensor_tensor(hb_rest[:, 1, :], hb_rest[:, 0, :], hb_split[:, 1, :], ALU.subtract
                                  ).then_inc(S["hb_small"], 1)
                dve.wait_ge(S["hb_small"], 4)
                dve.tensor_copy(hb_split[:, 2, :], hb_rest[:, 1, :]).then_inc(S["hb_small"], 1)

            for n in range(3):
                weight_parts(n)

            def iteration(g, par, n):
                qkv, att, gat = parts(n)

                def lo_part(parts_, source, at, name_hi, count, name_lo):
                    dve.wait_ge(S[name_hi], count)
                    dve.tensor_tensor(parts_[1][:, :, at], source[:, 0:D].rearrange("p (c n) -> p c n", c=C),
                                      parts_[0][:, :, at].bitcast(F32), ALU.subtract).then_inc(S[name_lo], 1)

                def evacuate_q(m):
                    dve.wait_ge(S["q_made"], 3 * g + m + 1)
                    dve.tensor_scalar(qT[:, par, m, :], ps_b[:], D0 ** -0.5, bq8[:, m:m + 1], ALU.mult, ALU.add
                                      ).then_inc(S["qk_b_ready"], 1)

                def evacuate_k(m):
                    dve.wait_ge(S["k_made"], 3 * g + m + 1)
                    dve.tensor_scalar(kT[:, par, m, :], ps_b[:], bk_col[:, m:m + 1], None, ALU.add
                                      ).then_inc(S["qk_b_ready"], 1)

                def turned_p1(t, q):
                    dve.wait_ge(S["p1_turned"], 3 * t + q + 1)
                    if due(t):
                        dve.wait_ge(S["ph_made"], t)
                    dve.tensor_copy(p1T[:, 4 * q:4 * q + 4, :], ps_d[:, q, :].rearrange("p (a n) -> p a n", a=4)
                                    ).then_inc(S[f"p1T_{q}"], 1)

                def evacuate_v(j):
                    dve.wait_ge(S["v_made"], G * g + j + 1)
                    dve.tensor_copy(v[:, par, j, :], ps_b[:, 0:D]).then_inc(S["v_odd"], 1)

                for j in range(G):
                    ta, tl = G * (g - 1) + j, G * (g - 2) + j
                    tt = tl - 1
                    tail = has_tail(n, j)
                    if att:
                        dve.wait_ge(S["scores_ready"], ta + 1)
                        dve.tensor_reduce(max0.rearrange("p (o i) -> p o i", o=2),
                                          ps_s[:, :, 0:C * N].rearrange("p o (i n) -> p o i n", i=C),
                                          AX_X, ALU.max).then_inc(S["att_small"], 1)
                        dve.wait_ge(S["att_small"], ta + 1)
                        if due(ta):
                            dve.wait_ge(S["exp0_ready"], ta)
                        dve.tensor_scalar(neg0, max0, -1.0, None, ALU.mult).then_inc(S["neg_ready"], 1)
                    if n == 0 and j == 3:
                        dve.wait_ge(S["bvf_made"], 1)
                        dve.tensor_tensor(bf_all[:], ps_s[:, 0, 0:D], bf_in, ALU.add).then_inc(S["bf_ready"], 1)
                    if gat:
                        lo_part(x1T, ps_b, slice(0, N), "x1_hi", tl + 1, "x1_lo")
                    if has_tail(n, j, 2):
                        t2 = tl - 2
                        dve.wait_ge(S["exp1_ready"], 3 * (t2 + 1))
                        dve.reciprocal(inv1, sum1).then_inc(S["inv1_ready"], 1)
                        dve.wait_ge(S["inv1_ready"], t2 + 1)
                        dve.wait_ge(S["f_turned"], t2 + 1)
                        if due(t2):
                            dve.wait_ge(S["tail_small"], 3 * (t2 - 1) + 1)
                        dve.tensor_tensor(f[:], ps_c[:, 0:D].rearrange("p (a e) -> p a e", a=H1),
                                          inv1.unsqueeze(2).broadcast_to([P, H1, D1]), ALU.mult
                                          ).then_inc(S["f0_ready"], 1)
                    if qkv and j == 3:
                        evacuate_v(1)
                    if tail:
                        dve.wait_ge(S["z_ready"], 3 * (tt + 1))
                        dve.tensor_reduce(zmax[:, 0:8], z[:, 0:8, :], AX_X, ALU.max).then_inc(S["zmax_ready"], 1)
                    if att:
                        dve.wait_ge(S["exp0_ready"], ta + 1)
                        if due(ta):
                            dve.wait_ge(S["p0_ready"], ta)
                        dve.reciprocal(inv0, sum0).then_inc(S["inv0_ready"], 1)
                    if tail:
                        dve.tensor_reduce(zmax[:, 8:12], z[:, 8:12, :], AX_X, ALU.max).then_inc(S["zmax_ready"], 1)
                        dve.wait_ge(S["zmax_ready"], 2 * (tt + 1))
                        if due(tt):
                            dve.wait_ge(S["exp1_ready"], 3 * tt)
                        dve.tensor_scalar(neg1, zmax, -1.0, None, ALU.mult).then_inc(S["neg1_ready"], 1)
                    if has_tail(n, j, 2):
                        t2 = tl - 2
                        flat = lambda w: w[:].rearrange("p a e -> p (a e)")
                        x1_ = x1[:, par if j > 1 else 1 - par, (j - 2) % G, :]
                        dve.wait_ge(S["fe_ready"], t2 + 1)
                        if due(t2):
                            dve.wait_ge(S["y_ready"], t2)
                        dve.scalar_tensor_tensor(r1[:], fe[:], 1.0, flat(f), ALU.min, ALU.max
                                                 ).then_inc(S["tail_small"], 1)
                        dve.wait_ge(S["tail_small"], 3 * t2 + 1)
                        dve.scalar_tensor_tensor(r1[:], r1[:], -1.0, x1_, ALU.add, ALU.subtract
                                                 ).then_inc(S["tail_small"], 1)
                        dve.wait_ge(S["tail_small"], 3 * t2 + 2)
                        dve.scalar_tensor_tensor(r1[:], gate[:, j % 2, :], 1.0, r1[:], ALU.add, ALU.mult
                                                 ).then_inc(S["tail_small"], 1)
                    if att:
                        dve.wait_ge(S["p0_turned"], ta + 1)
                        if due(ta):
                            dve.wait_ge(S["ctx_made"], ta)
                        dve.tensor_copy(p0T[:, 1, :, :], ps_s[:, 1, 0:C * N].rearrange("p (i n) -> p i n", i=C)
                                        ).then_inc(S["p0T_odd"], 1)
                    if gat:
                        dve.wait_ge(S["th_ready"], tl + 1)
                        if due(tl - 1):
                            dve.wait_ge(S["ph_made"], tl - 1)
                        dve.tensor_copy(h[:, j % 2, :, 0:D1], ps_d[:, 1, 0:D].rearrange("p (a e) -> p a e", a=H1)
                                        ).then_inc(S["h_ready"], 1)
                    if gat:
                        dve.wait_ge(S["thw_ready"], tl + 1)
                        dve.tensor_reduce(sd[:], thw[:].rearrange("p s (a e) -> p s a e", a=H1), AX_X,
                                          ALU.add).then_inc(S["sd_ready"], 1)
                    if n == 0 and j == 0:
                        small_constants()
                    if qkv and j == 0:
                        evacuate_q(1)
                    elif qkv and j == 1:
                        evacuate_k(0)
                    elif qkv and j == 2:
                        evacuate_k(2)
                    elif qkv:
                        evacuate_v(3)
                    if n == 0 and j < 3:
                        weight_parts(3 + j)
                    if att:
                        dve.wait_ge(S["ctx_made"], ta + 1)
                        lo_part(ctxT, ps_a, slice(0, N), "ctx_hi", ta + 1, "ctx_lo")
                    if gat:
                        dve.wait_ge(S["sd_ready"], tl + 1)
                        if due(tl):
                            dve.wait_ge(S["sd_turned"], tl)
                        dve.tensor_copy(sd3[:, :, 0, :], sd[:]).then_inc(S["split_small"], 1)
                        dve.wait_ge(S["split_small"], 4 * tl + 1)
                        dve.tensor_tensor(sd_rest[:, 0, :, :], sd[:], sd3[:, :, 0, :], ALU.subtract
                                          ).then_inc(S["split_small"], 1)
                        dve.wait_ge(S["split_small"], 4 * tl + 2)
                        dve.tensor_copy(sd3[:, :, 1, :], sd_rest[:, 0, :, :]).then_inc(S["split_small"], 1)
                        dve.wait_ge(S["split_small"], 4 * tl + 3)
                        dve.tensor_tensor(sd_rest[:, 1, :, :], sd_rest[:, 0, :, :], sd3[:, :, 1, :], ALU.subtract
                                          ).then_inc(S["split_small"], 1)
                        dve.wait_ge(S["split_small"], 4 * tl + 4)
                        dve.tensor_copy(sd3[:, :, 2, :], sd_rest[:, 1, :, :]).then_inc(S["sd3_ready"], 1)
                    if tail:
                        turned_p1(tt, 0)
                    if tail:
                        turned_p1(tt, 2)
                    if has_tail(n, j, 2):
                        t2 = tl - 2
                        dve.wait_ge(S["tail_small"], 3 * t2 + 3)
                        dve.scalar_tensor_tensor(r1[:], r1[:], 0.25, x1_, ALU.mult, ALU.add).then_inc(S["r1_ready"], 1)
                        dve.wait_ge(S["r1_ready"], t2 + 1)
                        dve.bn_stats(st1, r1[:]).then_inc(S["mv1_ready"], 1)
                        dve.wait_ge(S["mv1_ready"], apart(dve, 2 * t2 + 1))
                        dve.bn_aggr(mv1, st1).then_inc(S["mv1_ready"], 1)
                    if att:
                        dve.wait_ge(S["out_made"], ta + 1)
                        dve.wait_ge(S["xb_ready"], 2 * (g - 1) + j // 2 + 1)
                        if due(ta):
                            dve.wait_ge(S["x1_ready"], ta)
                        dve.tensor_tensor(r0[:], ps_b[:, 0:D], xb[:, 1 - par, j, :], ALU.add).then_inc(S["r0_ready"], 1)
                        dve.wait_ge(S["r0_ready"], ta + 1)
                        dve.bn_stats(st0, r0[:]).then_inc(S["mv0_ready"], 1)
                        dve.wait_ge(S["mv0_ready"], apart(dve, 2 * ta + 1))
                        dve.bn_aggr(mv0, st0).then_inc(S["mv0_ready"], 1)
                    if gat:
                        for q in range(3):
                            dve.wait_ge(S["relu_ready"], 3 * tl + q + 1)
                            dve.scalar_tensor_tensor(z[:, 4 * q:4 * q + 4, :],
                                                     ps_d[:, q, :].rearrange("p (a n) -> p a n", a=4), 0.2,
                                                     z[:, 4 * q:4 * q + 4, :], ALU.mult, ALU.add
                                                     ).then_inc(S["z_ready"], 1)
            pipeline(dve, iteration)

        @block_.gpsimd
        def _(pool):
            def x_lo(g, half):
                at = slice(2 * half * N, 2 * (half + 1) * N)
                pool.wait_ge(S["x_hi"], 2 * g + half + 1)
                pool.tensor_tensor(xT[1][:, :, at], x_cols[:, :, at], xT[0][:, :, at].bitcast(F32), ALU.subtract
                                   ).then_inc(S["x_lo"], 1)

            pool.memset(minus_half[:], -0.5)
            pool.memset(ones_b[:], 1.0)
            pool.memset(minus_one[:], -1.0).then_inc(S["minus_one_ready"], 1)
            pool.wait_ge(S["adj_in"], 16)
            for s in range(4):
                quarter = slice(B // 4 * s, B // 4 * (s + 1))
                pool.tensor_scalar(mask[:, quarter, :], adj_u8[:, quarter, :], 1.0, -1.0, ALU.mult, ALU.add
                                   ).then_inc(S["mask_ready"], 1)
            pool.wait_ge(S["hb_small"], 5)
            pool.dma_start(hb_rows[:], hb_split[:]).then_inc(S["hb_moved"], 16)
            pool.wait_ge(S["const_in"], 16 * 7)
            pool.tensor_scalar(b1_all[:], b1_all[:], 1.0, None, ALU.add).then_inc(S["b1_ready"], 1)

            def normalise(r, mv, ve, rs, nm, eps, out_ap, small, count, done, ready):
                pool.tensor_scalar(ve, mv[:, 1:2], eps, None, ALU.add).then_inc(S[small], 1)
                pool.wait_ge(S[small], count + 1)
                pool.tensor_tensor(rs, ve, minus_half[:], ALU.pow).then_inc(S[small], 1)
                pool.wait_ge(S[small], apart(pool, count + 2))
                pool.tensor_scalar(nm, mv[:, 0:1], -1.0, None, ALU.mult).then_inc(S[small], 1)
                pool.wait_ge(S[small], apart(pool, count + 3))
                pool.tensor_scalar(out_ap, r, nm, rs, ALU.add, ALU.mult).then_inc(S[ready], 1)

            def iteration(g, par, n):
                qkv, att, gat = parts(n)
                for j in range(G):
                    ta, tl = G * (g - 1) + j, G * (g - 2) + j
                    tt = tl - 1
                    tail = has_tail(n, j)
                    if has_tail(n, j, 2):
                        if n == 2:
                            pool.wait_ge(S["b1_ready"], 1)
                        pool.wait_ge(S["f0_ready"], tl - 1)
                        pool.tensor_tensor(f[:], f[:], b1_all[:].unsqueeze(1).broadcast_to([P, H1, D1]), ALU.add
                                           ).then_inc(S["f1_ready"], 1)
                    if att:
                        pool.wait_ge(S["inv0_ready"], ta + 1)
                        pool.tensor_tensor(p0[:].rearrange("p o i n -> p (o i) n"),
                                           p0[:].rearrange("p o i n -> p (o i) n"),
                                           inv0.unsqueeze(2).broadcast_to([P, H0, N]), ALU.mult
                                           ).then_inc(S["p0_ready"], 1)
                    if gat:
                        pool.wait_ge(S["th_ready"], tl + 1)
                        if due(tl):
                            pool.wait_ge(S["sd_ready"], tl)
                        pool.tensor_tensor(thw[:], th[:].unsqueeze(1).broadcast_to([P, 2, D]), w_sd[:], ALU.mult
                                           ).then_inc(S["thw_ready"], 1)
                    if qkv and n + 1 < NG and j == 3:
                        x_lo(g + 1, 0)
                        x_lo(g + 1, 1)
                    if qkv and j in (1, 2):
                        at = slice(2 * j - 2, 2 * j)
                        pool.wait_ge(S["xb_in"], 16 * (g + 1))
                        if n == 0:
                            pool.wait_ge(S["bf_ready"], 1)
                        pool.tensor_tensor(xb[:, par, at, :], xb[:, par, at, :],
                                           bf_all[:].unsqueeze(1).broadcast_to([P, 2, D]), ALU.add
                                           ).then_inc(S["xb_ready"], 1)
                    if has_tail(n, j, 2):
                        t2 = tl - 2
                        pool.wait_ge(S["mv1_ready"], apart(pool, 2 * t2 + 2))
                        if due(16 * (2 * (g - 2) + (j - 2) // 2)):
                            pool.wait_ge(S[f"y_stored_{j % 2}"], apart(pool, 16 * (2 * (g - 2) + (j - 2) // 2)))
                        normalise(r1[:], mv1, ve1, rs1, nm1, EPS / 4, y[:, j % 2, :], "ln1_small", 3 * t2, None,
                                  "y_ready")
                    if att:
                        pool.wait_ge(S["mv0_ready"], apart(pool, 2 * ta + 2))
                        if due(ta - 7):
                            pool.wait_ge(S["r1_ready"], apart(pool, ta - 7))
                        normalise(r0[:], mv0, ve0, rs0, nm0, EPS, x1[:, 1 - par, j, :], "ln0_small", 3 * ta, None,
                                  "x1_ready")
            pipeline(pool, iteration)


def kernel(**inputs):
    import numpy as _np
    import concourse.bacc as _bacc
    from concourse import mybir as _mybir
    from concourse.bass_utils import run_bass_kernel_spmd as _run

    nc = _bacc.Bacc("TRN2", target_bir_lowering=False, num_devices=1)
    names = ["x", "adj"] + ["L0_gnn_" + n for n in ("Wq", "bq", "Wk", "bk", "Wv", "bv", "Wf", "bf")] + [
        "L1_gnn_" + n for n in ("W", "b", "w_src", "w_dst", "H_w", "H_b")]
    x_ = _np.asarray(inputs["x"])
    held = {"xT": x_.reshape(NG, G, N, C, P).transpose(0, 4, 3, 1, 2).reshape(NG, P, C, G * N)}
    held.update({n: _np.asarray(inputs[n]) for n in names})
    held["L1_gnn_H_w"] = held["L1_gnn_H_w"].T
    held["L1_gnn_W"] = held["L1_gnn_W"].transpose(1, 0, 2).reshape(D, D)
    for n in ("L1_gnn_w_src", "L1_gnn_w_dst"):
        held[n] = held[n].reshape(D)
    for n in ("L0_gnn_bq", "L0_gnn_bk", "L0_gnn_bv"):
        held[n] = held[n].reshape(C, P).T
    held["ident"] = _np.eye(P, dtype=_np.float32)
    row = _np.arange(3 * H1)[:, None, None] % H1
    held["pick"] = _np.broadcast_to(row == _np.arange(H1)[None, :, None], (3 * H1, H1, P)).astype(_np.float32)
    arrays, args = {}, []
    for name, a in held.items():
        a = _np.ascontiguousarray(a)
        arrays[f"in_{name}_dram"] = a
        args.append(nc.dram_tensor(f"in_{name}_dram", a.shape, _mybir.dt.from_np(a.dtype), kind="ExternalInput").ap())
    out = nc.dram_tensor("out_0_dram", (B, N, D), F32, kind="ExternalOutput").ap()
    build_program(nc, *args, out)
    r = _run(nc, [arrays], core_ids=[0])
    return r.results[0]["out_0_dram"]
```
